# Optimizing a Trainium2 kernel written in Bass

```python
import numpy as np
import jax
import jax.numpy as jnp

def _softmax(x, axis=-1):
    return jax.nn.softmax(x, axis=axis)

def _gelu(x):
    return jax.nn.gelu(x, approximate=True)

def _silu(x):
    return jax.nn.silu(x)

def _sigmoid(x):
    return jax.nn.sigmoid(x)

def _layernorm(x, axis=-1, eps=1e-05):
    m = jnp.mean(x, axis=axis, keepdims=True)
    v = jnp.var(x, axis=axis, keepdims=True)
    return (x - m) / jnp.sqrt(v + eps)

def _scatter_add(tgt, idx, src, axis=0):
    return tgt.at[idx].add(src)

def _segment_sum(src, seg, n):
    return jax.ops.segment_sum(src, seg, n)
kernel_name = 'mk_metaformer_d1_conv_nchw128_r4_4e395d'

def setup_inputs(seed: int=0):
    np.random.seed(seed)
    _w = jnp.asarray

    def _rec_inputs():
        import jax
        import jax.numpy as jnp
        _gk = jax.random.key(seed)
        x = -7.109e-05 + 0.9999 * jax.random.normal(jax.random.fold_in(_gk, 1), (8, 32, 64, 64), jnp.float32)
        return x
    x = _rec_inputs()

    def _L0_conv_setup():
        import jax, jax.numpy as jnp
        import numpy as np
        HEADS = 4
        WS = 8
        EPS = 1e-06
        key = jax.random.key(seed)
        k1, k2, k3 = jax.random.split(key, 3)
        B, C, H, W = (8, 32, 64, 64)
        x = jax.random.normal(k1, (B, C, H, W), dtype=jnp.float32)
        norm_w = jnp.ones((C,), dtype=jnp.float32)
        norm_b = jnp.zeros((C,), dtype=jnp.float32)
        qkv_w = jax.random.normal(k2, (3 * C, C), dtype=jnp.float32) * C ** (-0.5)
        qkv_b = jnp.zeros((3 * C,), dtype=jnp.float32)
        proj_w = jax.random.normal(k3, (C, C), dtype=jnp.float32) * C ** (-0.5)
        proj_b = jnp.zeros((C,), dtype=jnp.float32)
        return {'x': x, 'norm_w': norm_w, 'norm_b': norm_b, 'qkv_w': qkv_w, 'qkv_b': qkv_b, 'proj_w': proj_w, 'proj_b': proj_b}
    _L0_conv_all = _L0_conv_setup()
    _L0_conv_in = {k: v for k, v in _L0_conv_all.items() if k in ('norm_w', 'norm_b', 'qkv_w', 'qkv_b', 'proj_w', 'proj_b')}
    del _L0_conv_all

    def _L0_ffn_setup():
        import jax, jax.numpy as jnp
        import numpy as np
        B, N, D, C, E, K = (8, 2048, 32, 32, 8, 2)
        key = jax.random.key(seed)
        k0, k1, k2 = jax.random.split(key, 3)
        x = jax.random.normal(k0, (B, N, D), dtype=jnp.float32)
        router_w = jax.random.normal(k1, (D, E), dtype=jnp.float32) * 0.05
        router_b = jnp.zeros((E,), dtype=jnp.float32)
        expert_w = jax.random.normal(k2, (E, D, C), dtype=jnp.float32) * (1.0 / np.sqrt(D))
        expert_b = jnp.zeros((E, C), dtype=jnp.float32)
        return {'x': x, 'router_w': router_w, 'router_b': router_b, 'expert_w': expert_w, 'expert_b': expert_b}
    _L0_ffn_all = _L0_ffn_setup()
    _L0_ffn_in = {k: v for k, v in _L0_ffn_all.items() if k in ('router_w', 'router_b', 'expert_w', 'expert_b')}
    del _L0_ffn_all
    return {'x': x, 'L0_conv_norm_w': _L0_conv_in['norm_w'], 'L0_conv_norm_b': _L0_conv_in['norm_b'], 'L0_conv_qkv_w': _L0_conv_in['qkv_w'], 'L0_conv_qkv_b': _L0_conv_in['qkv_b'], 'L0_conv_proj_w': _L0_conv_in['proj_w'], 'L0_conv_proj_b': _L0_conv_in['proj_b'], 'L0_ffn_router_w': _L0_ffn_in['router_w'], 'L0_ffn_router_b': _L0_ffn_in['router_b'], 'L0_ffn_expert_w': _L0_ffn_in['expert_w'], 'L0_ffn_expert_b': _L0_ffn_in['expert_b']}

def reference(x, L0_conv_norm_w, L0_conv_norm_b, L0_conv_qkv_w, L0_conv_qkv_b, L0_conv_proj_w, L0_conv_proj_b, L0_ffn_router_w, L0_ffn_router_b, L0_ffn_expert_w, L0_ffn_expert_b):
    import jax
    import jax.numpy as jnp

    def _L0_conv_ref(x, norm_w, norm_b, qkv_w, qkv_b, proj_w, proj_b):
        import jax, jax.numpy as jnp
        import numpy as np
        HEADS = 4
        WS = 8
        EPS = 1e-06
        B, C, H, W = x.shape
        heads, ws = (HEADS, WS)
        d = C // heads
        Nh, Nw = (H // ws, W // ws)
        scale = d ** (-0.5)
        mean = x.mean(axis=(2, 3), keepdims=True)
        var = x.var(axis=(2, 3), keepdims=True)
        xn = (x - mean) / jnp.sqrt(var + EPS)
        xn = norm_w[None, :, None, None] * xn + norm_b[None, :, None, None]
        qkv = jnp.einsum('oc,bchw->bohw', qkv_w, xn) + qkv_b[None, :, None, None]
        q, k, v = jnp.split(qkv, 3, axis=1)

        def window(t):
            t = t.reshape(B, heads, d, Nh, ws, Nw, ws)
            t = t.transpose(0, 3, 5, 1, 4, 6, 2)
            return t.reshape(B, Nh, Nw, heads, ws * ws, d)
        qw, kw, vw = (window(q), window(k), window(v))
        attn = jax.nn.softmax(jnp.einsum('...qd,...kd->...qk', qw, kw) * scale, axis=-1)
        out = jnp.einsum('...qk,...kd->...qd', attn, vw)
        out = out.reshape(B, Nh, Nw, heads, ws, ws, d)
        out = out.transpose(0, 3, 6, 1, 4, 2, 5).reshape(B, C, H, W)
        out = jnp.einsum('oc,bchw->bohw', proj_w, out) + proj_b[None, :, None, None]
        return out

    def _L0_ffn_ref(x, router_w, router_b, expert_w, expert_b):
        import jax, jax.numpy as jnp
        import numpy as np
        B, N, D, C, E, K = (8, 2048, 32, 32, 8, 2)
        router_probs = jax.nn.softmax(x @ router_w + router_b, axis=-1)
        top_p, top_i = jax.lax.top_k(router_probs, K)
        top_p = top_p / jnp.sum(top_p, axis=-1, keepdims=True)
        expert_out = jnp.einsum('bnd,edc->bnec', x, expert_w) + expert_b
        gathered = jnp.take_along_axis(expert_out, top_i[..., None], axis=2)
        return jnp.einsum('bnk,bnkc->bnc', top_p, gathered)

    def _gn(v, G=32, eps=1e-05):
        B_, C_, H_, W_ = v.shape
        g = v.reshape(B_, G, C_ // G, H_, W_)
        m = jnp.mean(g, axis=(2, 3, 4), keepdims=True)
        s = jnp.var(g, axis=(2, 3, 4), keepdims=True)
        return ((g - m) / jnp.sqrt(s + eps)).reshape(v.shape)

    def _ln_c(v, eps=1e-06):
        m = jnp.mean(v, axis=1, keepdims=True)
        s = jnp.var(v, axis=1, keepdims=True)
        return (v - m) / jnp.sqrt(s + eps)

    def _ln_t(v, eps=1e-05):
        m = jnp.mean(v, axis=-1, keepdims=True)
        s = jnp.var(v, axis=-1, keepdims=True)
        return (v - m) / jnp.sqrt(s + eps)

    def _to_tokens(v):
        B_, C_, H_, W_ = v.shape
        return v.reshape(B_, C_, H_ * W_).transpose(0, 2, 1)

    def _from_tokens(t, like):
        B_, C_, H_, W_ = like.shape
        return t.transpose(0, 2, 1).reshape(B_, C_, H_, W_)
    x = x + _L0_conv_ref(_ln_c(x), L0_conv_norm_w, L0_conv_norm_b, L0_conv_qkv_w, L0_conv_qkv_b, L0_conv_proj_w, L0_conv_proj_b)
    t = _to_tokens(x)
    t = t + _L0_ffn_ref(_ln_t(t), L0_ffn_router_w, L0_ffn_router_b, L0_ffn_expert_w, L0_ffn_expert_b)
    x = _from_tokens(t, x)
    return x

_drawn_inputs = setup_inputs


def setup_inputs(seed=0):
    import zlib

    import numpy as np

    out = dict(_drawn_inputs(seed))
    spreads = {'L0_conv_norm_w': (1.0, 0.2),
     'L0_conv_norm_b': (0.0, 0.1),
     'L0_conv_qkv_b': (0.0, 0.1),
     'L0_conv_proj_b': (0.0, 0.1),
     'L0_ffn_router_b': (0.0, 0.1),
     'L0_ffn_expert_b': (0.0, 0.1)}
    factors = {}
    for name, (base, spread) in spreads.items():
        noise = np.random.default_rng([zlib.crc32(name.encode()), seed]).standard_normal(out[name].shape)
        drawn = base * np.exp(spread * noise) if base else spread * noise
        out[name] = jnp.asarray(drawn.astype(out[name].dtype))
    for name, factor in factors.items():
        out[name] = (out[name] * factor).astype(out[name].dtype)
    return out
```

```python
from contextlib import ExitStack

import concourse.bass as bass
from concourse import mybir

B, C, H, W = 8, 32, 64, 64
HEADS, WS, E = 4, 8, 8
D = C // HEADS
TOK = WS * WS
NW = W // WS
P = 128
IMG = P // C
GROUPS = B // IMG
CHUNK = WS * W
BANDS = H // WS
CHUNKS = GROUPS * BANDS
QUAD = 4
QUADS = CHUNKS // QUAD
PAIRS = IMG // 2
SPLITS = 3
SCALE = float(D) ** -0.5
EPS_CONV, EPS_FFN, EPS_INST = 1e-6, 1e-5, 1e-6
FAR = -3.0e38

F32 = mybir.dt.float32
BF16 = mybir.dt.bfloat16
ALU = mybir.AluOpType
ACT = mybir.ActivationFunctionType
AX = mybir.AxisListType


def metaformer_block(nc, io):
    x_v = io["x"].rearrange("(g b) c y x -> g (b c) (y x)", b=IMG)
    out_v = io["out"].rearrange("(g b) c (n y) x -> (b c) g n (y x)", b=IMG, y=WS)

    with ExitStack() as ctx:
        def sb(name, shape, dt=F32):
            return ctx.enter_context(nc.sbuf_tensor(name, shape, dt))

        def sem(name):
            return ctx.enter_context(nc.semaphore(name))

        stage = sb("stage", [P, CHUNKS * CHUNK])
        x_win = sb("x_win", [P, CHUNKS * CHUNK])
        act_all = sb("act_all", [P, CHUNKS * CHUNK])
        half = 2 * IMG * CHUNK
        q_head = stage[:, 0:half].rearrange("p (u h n) -> p u h n", u=2, h=HEADS)
        k_img = stage[:, half:2 * half].rearrange("p (u win b t) -> p u win b t", u=2, win=NW, b=IMG)
        x_rep = stage[:, 0:half].rearrange("p (u b n) -> p u b n", u=2, b=IMG)
        t_norm = stage[:, half:2 * half].rearrange("p (u j n) -> p u j n", u=2, j=QUAD)
        work = sb("work", [P, 2 * IMG * CHUNK])
        q_img = work[:, 0:IMG * CHUNK].rearrange("p (win b t) -> p win b t", win=NW, b=IMG)
        k_head = work[:, IMG * CHUNK:].rearrange("p (h n) -> p h n", h=HEADS)
        centred = work[:, :].rearrange("p (u j n) -> p u j n", u=2, j=QUAD)
        v_cols = sb("v_cols", [P, 2, NW * PAIRS * HEADS, 2, 2, D])
        v_flat = v_cols[:].rearrange("p u g b n d -> p (u g b n d)")
        late = sb("late", [P, QUAD * CHUNK])
        squares = late[:, :].rearrange("p (j n) -> p j n", j=QUAD)
        std = sb("std", [P, CHUNK])
        rstd = sb("rstd", [P, CHUNK])
        stats = sb("stats", [P, CHUNKS, 6])
        moments = sb("moments", [P, GROUPS, 2])
        inst = sb("inst", [P, 4, GROUPS])
        inst_s = sb("inst_s", [P, CHUNKS])
        inst_t = sb("inst_t", [P, CHUNKS])
        x_cur = sb("x_cur", [P, 2, CHUNK])
        q_sb = sb("q_sb", [P, CHUNK])
        k_sb = sb("k_sb", [P, CHUNK])
        neg_max = sb("neg_max", [P, NW * PAIRS * HEADS])
        max_rest = sb("max_rest", [NW * PAIRS * HEADS, P])
        max_parts = sb("max_parts", [NW * PAIRS * HEADS, SPLITS, P], BF16)
        rows = sb("rows", [P, NW * PAIRS * HEADS * TOK])
        max_rows = rows[:, :].bitcast(BF16).rearrange("p (u n) -> p u n", u=2)
        probs = late[:, :].rearrange("p (s n) -> p s n", s=4)
        o_tok = sb("o_tok", [P, 2, 16, 32])
        o_rden = sb("o_rden", [P, 2, 32])
        o_norm = sb("o_norm", [P, 2, 8, 32])
        o_chan = sb("o_chan", [P, CHUNK])
        gate_parts = sb("gate_parts", [P, SPLITS, CHUNK], BF16)
        gate_rows = sb("gate_rows", [P, QUAD, CHUNK], BF16)
        scaled = rows[:, 0:2 * CHUNK].rearrange("p (u n) -> p u n", u=2)
        out_sb = rows[:, 2 * CHUNK:4 * CHUNK].rearrange("p (u n) -> p u n", u=2)

        def g3(k):
            return v_flat[:, k * CHUNK:(k + 1) * CHUNK].rearrange("p (g e) -> p g e", e=E)

        logit, logit_t, g_a, g_b, g_mask1, g_mask2, g_rest, gate_t = (
            v_flat[:, k * CHUNK:(k + 1) * CHUNK] for k in range(8))
        small = sb("small", [P, 6, CHUNK // E])
        g_diff, g_exp, gate_f32 = (rows[:, k * CHUNK:(k + 1) * CHUNK] for k in range(4, 7))

        const = {n: sb("sb_" + n, list(a.shape)) for n, a in io.items() if n.startswith("c_")}
        ones_in, gate_in = q_sb[:, 0:P], x_cur[:, :, :].rearrange("p u n -> p (u n)")
        ones_sel = sb("ones_sel", [P, P], BF16)
        gate_sel = sb("gate_sel", [P, 2 * IMG * P], BF16)
        qb_scaled = sb("qb_scaled", [P, 1])
        proj_bias = sb("proj_bias", [P, 1])

        bank = [ctx.enter_context(nc.psum_tensor(f"bank{i}", [P, 512], F32)) for i in range(8)]

        x_loaded = [sem(f"x_loaded{g}") for g in range(GROUPS)]
        consts_loaded = sem("consts_loaded")
        filled = sem("filled")
        x_win_ready = sem("x_win_ready")

        def norm_sems(tag):
            return {n: sem(f"{tag}_{n}") for n in
                    ("centred_ps", "squared", "var_ps", "std_ready", "rstd_ready", "rstd_ps", "normed")}

        ln1, ln2 = norm_sems("ln1"), norm_sems("ln2")
        stats_done = sem("stats_done")
        inst_step = sem("inst_step")
        inst_std = sem("inst_std")
        affine_ready = sem("affine_ready")
        bias_ps = sem("bias_ps")
        biases_ready = sem("biases_ready")
        x_cur_ready = sem("x_cur_ready")
        q_ps = sem("q_ps")
        k_ps = sem("k_ps")
        v_ps = sem("v_ps")
        q_done = sem("q_done")
        k_done = sem("k_done")
        v_done = sem("v_done")
        rank_masks = sem("rank_masks")
        score_masks = sem("score_masks")
        rank_ps = sem("rank_ps")
        max_done = sem("max_done")
        max_t_ps = sem("max_t_ps")
        max_split = sem("max_split")
        max_rows_in = sem("max_rows_in")
        score_ps = sem("score_ps")
        exp_done = sem("exp_done")
        pv_ps = sem("pv_ps")
        o_turned = sem("o_turned")
        o_recip = sem("o_recip")
        o_normed = sem("o_normed")
        o_back = sem("o_back")
        proj_ps = sem("proj_ps")
        x2_done = sem("x2_done")
        logits_ps = sem("logits_ps")
        gate_step = sem("gate_step")
        gate_diff = sem("gate_diff")
        gate_part = sem("gate_part")
        gate_exp = sem("gate_exp")
        gates_in = sem("gates_in")
        x_rep_in = [sem(f"x_rep_in{u}") for u in range(2)]
        gate_ps = sem("gate_ps")
        scaled_done = sem("scaled_done")
        y_step = sem("y_step")
        summed = sem("summed")
        stored = sem("stored")
        out_free = sem("out_free")

        XC, NORMED, V, X2, S, EXP, PV, OT, MX, SC, Y, SUM, OUT, ONE = 2, 8, 2, 2, 16, 2, 4, 2, 2, 2, 2, 2, 2, 1
        GATE_OPS = 20

        block = ctx.enter_context(nc.Block())

        @block.sync
        def _(sp):
            for g in range(GROUPS):
                sp.dma_start(stage[:, g * BANDS * CHUNK:(g + 1) * BANDS * CHUNK], x_v[g]).then_inc(x_loaded[g], 16)

            def move_max(m, u):
                split_all, scores_used = sp.snap(m * 4 + 4), sp.snap(m * NW + 8)
                sp.wait_ge(max_split, split_all)
                sp.wait_ge(score_ps, scores_used)
                for b in range(2):
                    for s in range(SPLITS):
                        sp.dma_start(max_rows[b * SPLITS + s:b * SPLITS + s + 1, u, :],
                                     max_parts[:, s, b * TOK:(b + 1) * TOK]).then_inc(max_rows_in, 16)

            move_max(0, 0)
            with sp.Fori(0, CHUNKS // 2 - 1) as i:
                move_max(i * 2 + 1, 1)
                move_max(i * 2 + 2, 0)
            move_max(CHUNKS - 1, 1)

            with sp.Fori(0, QUADS // 2) as i:
                for u in range(2):
                    quad = i * 2 + u
                    split_all, used = sp.snap(quad * GATE_OPS + (GATE_OPS + ONE)), sp.snap(quad * (8 * QUAD) + Y)
                    done = [sp.snap(quad * QUAD + (j + 1)) for j in range(QUAD)]
                    sp.wait_ge(gate_step, split_all)
                    sp.wait_ge(y_step, used)
                    for j in range(QUAD):
                        for s in range(SPLITS):
                            sp.dma_start(gate_rows[32 * s:32 * s + 32, j, :],
                                         gate_parts[32 * j:32 * j + 32, s, :]).then_inc(gates_in, 16)
                    for j in range(QUAD):
                        sp.wait_ge(summed, done[j])
                        for b in range(IMG):
                            for e in range(IMG):
                                sp.dma_start(x_rep[32 * e:32 * e + 32, j % 2, b, :],
                                             t_norm[32 * b:32 * b + 32, u, j, :]).then_inc(x_rep_in[j % 2], 16)

        @block.gpsimd
        def _(pool):
            pool.sem_inc(out_free, OUT)
            for n in const:
                pool.dma_start(const[n][:], io[n]).then_inc(consts_loaded, 16)
            pool.dma_start(ones_in, io["s_ones"]).then_inc(consts_loaded, 16)
            pool.dma_start(gate_in, io["s_gate"]).then_inc(consts_loaded, 16)
            pool.memset(v_flat, 0.0).then_inc(filled, 1)
            pool.memset(rows[:, :], 0.0).then_inc(filled, 1)
            pool.memset(gate_rows[:, :, :], 0.0).then_inc(filled, 1)
            pool.wait_ge(filled, 3)
            for b in range(2):
                pool.memset(v_cols[b * 64:b * 64 + 64, :, :, b, 1, :].rearrange("p u g d -> p (u g) d"),
                            1.0).then_inc(filled, 1)
                pool.wait_ge(filled, 4 + b)
            for g in range(GROUPS):
                pool.wait_ge(x_loaded[g], 16)
                with pool.Fori(g * BANDS, (g + 1) * BANDS) as c:
                    pool.tensor_copy(
                        x_win[:, bass.ds(c * CHUNK, CHUNK)].rearrange("p (win y x) -> p win y x", win=NW, y=WS),
                        stage[:, bass.ds(c * CHUNK, CHUNK)].rearrange("p (y win x) -> p win y x", win=NW, y=WS),
                    ).then_inc(x_win_ready, 1)
            with pool.Fori(0, QUADS // 2) as i:
                for u in range(2):
                    for j in range(QUAD):
                        c = i * (2 * QUAD) + (u * QUAD + j)
                        pool.wait_ge(summed, c + 1 + SUM)
                        pool.dma_start(out_v[:, bass.ds(i, 1), u * QUAD + j, :].rearrange("p a n -> p (a n)"),
                                       out_sb[:, j % 2, :]).then_inc(stored, 16)
                        pool.wait_ge(stored, c * 16 + 16)
                        pool.sem_inc(out_free, 1)

        def norm_pe(pe, sems, quad, u, source, first_wait, bank2_free):
            for j in range(QUAD):
                c = quad * QUAD + j
                first_wait(c)
                pe.wait_ge(sems["squared"], c + 1)
                nc.tensor.matmul(bank[j % 2][:, :], const["c_centre"][:, :], source[:, bass.ds(c * CHUNK, CHUNK)],
                                 start=True, stop=True).then_inc(sems["centred_ps"], 1)
            for j in range(QUAD):
                if j == 0:
                    pe.wait_ge(sems["std_ready"], quad + ONE)
                    bank2_free()
                pe.wait_ge(sems["squared"], quad * QUAD + j + 1 + XC)
                last = nc.tensor.matmul(bank[2][32 * j:32 * j + 32, :], const["c_mean"][:, :], squares[:, j, :],
                                        start=True, stop=True)
            last.then_inc(sems["var_ps"], 1)
            for j in range(QUAD):
                if j == 0:
                    pe.wait_ge(sems["rstd_ready"], quad + 1 + ONE)
                pe.wait_ge(sems["normed"], quad * QUAD + j + NORMED)
                nc.tensor.matmul(bank[3][:, :], const["c_spread"][:, j, :], rstd[:, :],
                                 start=True, stop=True).then_inc(sems["rstd_ps"], 1)

        def norm_act(act, sems, quad, u, eps):
            for j in range(QUAD):
                c = quad * QUAD + j
                act.wait_ge(sems["centred_ps"], c + 1)
                act.wait_ge(sems["normed"], c + 1)
                nc.scalar.activation(centred[:, u, j, :], bank[j % 2][:, :], ACT.Copy)
                act.wait_ge(sems["var_ps"], quad + ONE)
                nc.scalar.activation(squares[:, j, :], bank[j % 2][:, :], ACT.Square).then_inc(sems["squared"], 1)
            act.wait_ge(sems["var_ps"], quad + 1 + ONE)
            act.wait_ge(sems["rstd_ready"], quad + ONE)
            nc.scalar.activation(std[:, :], bank[2][:, :], ACT.Sqrt, bias=eps).then_inc(sems["std_ready"], 1)

        def norm_dve(dve, sems, quad, u, target):
            dve.wait_ge(sems["std_ready"], quad + 1 + ONE)
            dve.wait_ge(sems["rstd_ps"], quad * QUAD + ONE)
            nc.vector.reciprocal(rstd[:, :], std[:, :]).then_inc(sems["rstd_ready"], 1)
            for j in range(QUAD):
                c = quad * QUAD + j
                dve.wait_ge(sems["rstd_ps"], c + 1 + ONE)
                dve.wait_ge(sems["squared"], c + 1 + XC)
                nc.vector.tensor_tensor(target(c, j), centred[:, u, j, :], bank[3][:, :],
                                        ALU.mult).then_inc(sems["normed"], 1)

        @block.tensor
        def _(pe):
            for s, k in ((v_ps, V), (proj_ps, ONE), (ln1["var_ps"], ONE), (ln2["var_ps"], ONE),
                         (ln1["rstd_ps"], ONE), (ln2["rstd_ps"], ONE)):
                pe.sem_inc(s, k)
            pe.sem_inc(score_ps, S)
            pe.sem_inc(pv_ps, PV)
            pe.sem_inc(y_step, Y)
            pe.wait_ge(consts_loaded, 16 * (len(const) + 2))
            nc.tensor.matmul(bank[7][:, 0:1], const["c_wp"][:, :], const["c_vb"][:, :],
                             start=True, stop=True).then_inc(bias_ps, 1)
            with pe.Fori(0, QUADS // 2) as i:
                for u in range(2):
                    norm_pe(pe, ln1, i * 2 + u, u, x_win,
                            lambda c: pe.wait_ge(x_win_ready, c + 1), lambda: None)

            def qkv(m, u, first=False):
                pe.wait_ge(x_cur_ready, m + 1)
                pe.wait_ge(x2_done, m + 1)
                nc.tensor.matmul(bank[0][:, :], const["c_wq"][:, :], x_cur[:, u, :],
                                 start=True, stop=True).then_inc(q_ps, 1)
                pe.wait_ge(q_done, m + 1)
                nc.tensor.matmul(bank[0][:, :], const["c_wk"][:, :], x_cur[:, u, :],
                                 start=True, stop=True).then_inc(k_ps, 1)
                if not first:
                    pe.wait_ge(max_split, m * 4 - 2)
                for w in range(NW):
                    for b in range(2):
                        last = nc.tensor.matmul(bank[1][64 * b:64 * b + 64, w * 64:w * 64 + 64],
                                                x_cur[:, u, w * TOK:w * TOK + TOK], const["c_wv"][:, b, :],
                                                start=True, stop=True)
                last.then_inc(v_ps, 1)

            def rank(m, w):
                pe.wait_ge(max_done, m * NW + w + 1)
                if w == 0:
                    pe.wait_ge(rank_masks, m + 1)
                for p in range(PAIRS):
                    last = nc.tensor.matmul(bank[2 + w % 2][:, p * 256:p * 256 + 256],
                                            q_img[:, w, 2 * p:2 * p + 2, :].rearrange("p b t -> p (b t)"),
                                            k_head[:, :, w * TOK:w * TOK + TOK], start=True, stop=True)
                last.then_inc(rank_ps, 1)

            def turn_max(m):
                pe.wait_ge(max_done, m * NW + NW + MX)
                pe.wait_ge(v_done, m * 2 + 2)
                nc.tensor.matmul(bank[1][0:64, 0:P], neg_max[:, :], const["c_ident"][:, :],
                                 start=True, stop=True).then_inc(max_t_ps, 1)

            def scores(n, u, w):
                if w == 0:
                    pe.wait_ge(score_masks, n + 1)
                    pe.wait_ge(max_rows_in, n * (2 * SPLITS * 16) + 2 * SPLITS * 16)
                pe.wait_ge(exp_done, n * NW + w + 1)
                t = bank[4 + w % 2]
                nc.tensor.matmul(t[:, :], ones_sel[:, :], max_rows[:, u, w * 512:w * 512 + 512],
                                 start=True, stop=False, skip_group_check=True)
                for p in range(PAIRS):
                    last = nc.tensor.matmul(t[:, p * 256:p * 256 + 256],
                                            k_img[:, u, w, 2 * p:2 * p + 2, :].rearrange("p b t -> p (b t)"),
                                            q_head[:, u, :, w * TOK:w * TOK + TOK],
                                            start=False, stop=(p == PAIRS - 1), skip_group_check=True)
                last.then_inc(score_ps, 1)

            def weigh(n, u, w):
                if w == 0:
                    pe.wait_ge(v_done, n * 2 + 2)
                if w % 4 == 0:
                    pe.wait_ge(o_turned, n * 2 + (w // 4 + 1))
                pe.wait_ge(exp_done, n * NW + w + 1 + EXP)
                for p in range(PAIRS):
                    for h in range(HEADS):
                        at = p * 256 + (w % 4) * TOK
                        last = nc.tensor.matmul(
                            bank[6 + w // 4][32 * h:32 * h + 32, at:at + TOK],
                            v_cols[:, u, (w * PAIRS + p) * HEADS + h, :, :, :].rearrange("p b n d -> p (b n d)"),
                            probs[:, w % 4, (p * HEADS + h) * TOK:(p * HEADS + h + 1) * TOK],
                            start=True, stop=True)
                last.then_inc(pv_ps, 1)

            def project(n, k_waits):
                pe.wait_ge(o_back, n * 2 + 2)
                pe.wait_ge(k_done, k_waits)
                nc.tensor.matmul(bank[0][:, :], const["c_wp"][:, :], o_chan[:, :],
                                 start=True, stop=True).then_inc(proj_ps, 1)

            def front(m, u):
                qkv(m, u, first=True)
                for w in range(NW):
                    rank(m, w)
                turn_max(m)

            def both(m, um, n, un):
                qkv(m, um)
                for w in range(NW):
                    scores(n, un, w)
                    if w >= 1:
                        weigh(n, un, w - 1)
                    if w >= 4:
                        rank(m, 2 * (w - 4))
                        rank(m, 2 * (w - 4) + 1)
                weigh(n, un, NW - 1)
                turn_max(m)
                project(n, n + 2)

            pe.wait_ge(biases_ready, 1)
            front(0, 0)
            with pe.Fori(0, CHUNKS // 2 - 1) as i:
                both(i * 2 + 1, 1, i * 2, 0)
                both(i * 2 + 2, 0, i * 2 + 1, 1)
            both(CHUNKS - 1, 1, CHUNKS - 2, 0)
            for w in range(NW):
                scores(CHUNKS - 1, 1, w)
                if w >= 1:
                    weigh(CHUNKS - 1, 1, w - 1)
            weigh(CHUNKS - 1, 1, NW - 1)
            project(CHUNKS - 1, CHUNKS)

            pe.wait_ge(x2_done, CHUNKS + X2)
            with pe.Fori(0, QUADS // 2) as i:
                for u in range(2):
                    quad = i * 2 + u
                    norm_pe(pe, ln2, quad, u, act_all, lambda c: None,
                            lambda: pe.wait_ge(gate_step, quad * GATE_OPS + ONE))
                    for j in range(QUAD):
                        c = quad * QUAD + j
                        pe.wait_ge(ln2["normed"], c + 1 + NORMED)
                        if j == 0:
                            pe.wait_ge(ln2["std_ready"], quad + 1 + ONE)
                        last = nc.tensor.matmul(bank[2][32 * j:32 * j + 32, :], const["c_router"][:, :],
                                                t_norm[:, u, j, :], start=True, stop=True)
                    last.then_inc(logits_ps, 1)
                    pe.wait_ge(gates_in, quad * (QUAD * SPLITS * 16) + QUAD * SPLITS * 16)
                    for j in range(QUAD):
                        c = quad * QUAD + j
                        y = bank[6 + j % 2]
                        pe.wait_ge(summed, c + 1)
                        nc.tensor.matmul(y[:, :], const["c_eb"][:, j, :], gate_f32,
                                         start=True, stop=False, skip_group_check=True)

                        def spread(k):
                            pe.wait_ge(scaled_done, c * 8 + (k + 1))
                            nc.tensor.matmul(bank[4 + k % 2][:, :], gate_sel[:, k * P:(k + 1) * P], gate_rows[:, j, :],
                                             start=True, stop=True).then_inc(gate_ps, 1)

                        def expert(k):
                            b, eh = k // 2, k % 2
                            pe.wait_ge(scaled_done, c * 8 + (k + 1 + SC))
                            mm = nc.tensor.matmul(y[32 * b:32 * b + 32, :], const["c_we"][:, eh, :],
                                                  scaled[:, k % 2, :], start=False, stop=(eh == 1),
                                                  skip_group_check=True)
                            mm.then_inc(y_step, 1)
                            return mm

                        spread(0)
                        for k in range(1, 2 * IMG):
                            spread(k)
                            expert(k - 1)
                        expert(2 * IMG - 1)

        @block.scalar
        def _(act):
            for sems in (ln1, ln2):
                act.sem_inc(sems["squared"], XC)
                act.sem_inc(sems["std_ready"], ONE)
            act.sem_inc(exp_done, EXP)
            with act.Fori(0, QUADS // 2) as i:
                for u in range(2):
                    norm_act(act, ln1, i * 2 + u, u, const["c_eps"][:, 0:1])
            act.wait_ge(inst_step, 2)
            nc.scalar.activation(inst[:, 0, :], moments[:, :, 1], ACT.Sqrt, bias=const["c_eps"][:, 2:3]
                                 ).then_inc(inst_std, 1)

            def current(m, u):
                if isinstance(m, int) and m == 0:
                    act.wait_ge(affine_ready, 1)
                act.wait_ge(v_ps, m + 1)
                nc.scalar.activation(x_cur[:, u, :], act_all[:, bass.ds(m * CHUNK, CHUNK)], ACT.Identity,
                                     bias=inst_t[:, bass.ds(m, 1)], scale=inst_s[:, bass.ds(m, 1)]
                                     ).then_inc(x_cur_ready, 1)

            def evacuate(m, u, first=False):
                act.wait_ge(q_ps, m + 1)
                act.wait_ge(score_masks, m)
                nc.scalar.activation(q_sb[:, :], bank[0][:, :], ACT.Identity, bias=qb_scaled[:, 0:1],
                                     scale=SCALE).then_inc(q_done, 1)
                act.wait_ge(v_ps, m + 1 + V)
                if not first:
                    act.wait_ge(pv_ps, m * NW - 4)
                else:
                    act.wait_ge(filled, 5)
                for b in range(2):
                    nc.scalar.activation(v_cols[64 * b:64 * b + 64, u, :, b, 0, :],
                                         bank[1][64 * b:64 * b + 64, :].rearrange("p (g d) -> p g d", d=D),
                                         ACT.Copy).then_inc(v_done, 1)

            def exps(n):
                for w in range(NW):
                    act.wait_ge(score_ps, n * NW + w + 1 + S)
                    act.wait_ge(pv_ps, n * NW + w + 1)
                    nc.scalar.activation(probs[:, w % 4, :], bank[4 + w % 2][:, :], ACT.Exp).then_inc(exp_done, 1)

            current(0, 0)
            evacuate(0, 0, first=True)
            current(1, 1)
            with act.Fori(0, CHUNKS // 2 - 1) as i:
                evacuate(i * 2 + 1, 1)
                exps(i * 2)
                current(i * 2 + 2, 0)
                evacuate(i * 2 + 2, 0)
                exps(i * 2 + 1)
                current(i * 2 + 3, 1)
            evacuate(CHUNKS - 1, 1)
            exps(CHUNKS - 2)
            exps(CHUNKS - 1)

            with act.Fori(0, QUADS // 2) as i:
                for u in range(2):
                    quad = i * 2 + u
                    norm_act(act, ln2, quad, u, const["c_eps"][:, 1:2])
                    act.wait_ge(gate_diff, quad + 1)
                    nc.scalar.activation(g_exp, g_diff, ACT.Exp).then_inc(gate_exp, 1)

        @block.vector
        def _(dve):
            for s, k in ((ln1["normed"], NORMED), (ln2["normed"], NORMED), (x2_done, X2), (o_turned, OT),
                         (max_done, MX), (scaled_done, SC), (summed, SUM), (gate_step, ONE),
                         (ln1["rstd_ready"], ONE), (ln2["rstd_ready"], ONE)):
                dve.sem_inc(s, k)
            dve.wait_ge(consts_loaded, 16 * (len(const) + 2))
            nc.vector.tensor_scalar(qb_scaled[:, :], const["c_qb"][:, :], SCALE, None, ALU.mult)
            nc.vector.tensor_copy(ones_sel[:, :], ones_in)
            nc.vector.tensor_copy(gate_sel[:, :], gate_in)
            dve.wait_ge(bias_ps, 1)
            nc.vector.tensor_tensor(proj_bias[:, :], bank[7][:, 0:1], const["c_pb"][:, :],
                                    ALU.add).then_inc(biases_ready, 1)
            with dve.Fori(0, QUADS // 2) as i:
                for u in range(2):
                    norm_dve(dve, ln1, i * 2 + u, u, lambda c, j: act_all[:, bass.ds(c * CHUNK, CHUNK)])
                    for j in range(QUAD):
                        c = (i * 2 + u) * QUAD + j
                        dve.wait_ge(ln1["normed"], c + 1 + NORMED)
                        nc.vector.bn_stats(stats[:, bass.ds(c, 1), :].rearrange("p a s -> p (a s)"),
                                           act_all[:, bass.ds(c * CHUNK, CHUNK)]).then_inc(stats_done, 1)
            dve.wait_ge(stats_done, CHUNKS)
            for g in range(GROUPS):
                nc.vector.bn_aggr(moments[:, g, :], stats[:, g * BANDS:(g + 1) * BANDS, :]
                                  .rearrange("p n s -> p (n s)")).then_inc(inst_step, 1)
            dve.wait_ge(inst_std, 1)
            nc.vector.reciprocal(inst[:, 1, :], inst[:, 0, :]).then_inc(inst_step, 1)
            dve.wait_ge(inst_step, 3)
            nc.vector.tensor_scalar(inst[:, 2, :], inst[:, 1, :], const["c_nw"][:, 0:1], None,
                                    ALU.mult).then_inc(inst_step, 1)
            dve.wait_ge(inst_step, 4)
            nc.vector.tensor_tensor(inst[:, 3, :], moments[:, :, 0], inst[:, 2, :], ALU.mult).then_inc(inst_step, 1)
            dve.wait_ge(inst_step, 5)
            for g in range(GROUPS):
                at = slice(g * BANDS, (g + 1) * BANDS)
                nc.vector.tensor_copy(inst_s[:, at], inst[:, 2, g:g + 1].to_broadcast([P, BANDS]))
                last = nc.vector.tensor_scalar(inst_t[:, at], inst[:, 3, g:g + 1].to_broadcast([P, BANDS]),
                                               -1.0, const["c_nb"][:, 0:1], ALU.mult, ALU.add)
            last.then_inc(affine_ready, 1)

            def keys(m):
                dve.wait_ge(k_ps, m + 1)
                dve.wait_ge(score_masks, m)
                nc.vector.tensor_scalar(k_sb[:, :], bank[0][:, :], const["c_kb"][:, 0:1], None,
                                        ALU.add).then_inc(k_done, 1)

            def masks(m, u):
                dve.wait_ge(q_done, m + 1)
                dve.wait_ge(k_done, m + 1)
                dve.wait_ge(rank_ps, m * NW)
                for b in range(IMG):
                    nc.vector.tensor_scalar(q_img[:, :, b, :], q_sb[:, :].rearrange("p (win t) -> p win t", win=NW),
                                            const["c_masks"][:, b:b + 1], None, ALU.mult)
                for h in range(HEADS):
                    last = nc.vector.tensor_scalar(k_head[:, h, :], k_sb[:, :],
                                                   const["c_masks"][:, IMG + h:IMG + h + 1], None, ALU.mult)
                last.then_inc(rank_masks, 1)
                dve.wait_ge(score_ps, m * NW + 8)
                for h in range(HEADS):
                    nc.vector.tensor_scalar(q_head[:, u, h, :], q_sb[:, :],
                                            const["c_masks"][:, IMG + h:IMG + h + 1], None, ALU.mult)
                for b in range(IMG):
                    last = nc.vector.tensor_scalar(k_img[:, u, :, b, :], k_sb[:, :].rearrange("p (win t) -> p win t", win=NW),
                                                   const["c_masks"][:, b:b + 1],
                                                   None, ALU.mult)
                last.then_inc(score_masks, 1)

            def maxima(m):
                for w in range(NW):
                    dve.wait_ge(rank_ps, m * NW + (w + 1))
                    nc.vector.tensor_reduce(neg_max[:, w * 8:w * 8 + 8],
                                            bank[2 + w % 2][:, :].rearrange("p (g k) -> p g k", k=TOK),
                                            AX.X, ALU.max, negate=True).then_inc(max_done, 1)

            def split_max(m, first=False):
                dve.wait_ge(max_t_ps, m + 1)
                if not first:
                    dve.wait_ge(max_rows_in, m * (2 * SPLITS * 16))
                t = bank[1][0:64, 0:P]
                nc.vector.tensor_copy(max_parts[:, 0, :], t).then_inc(max_split, 1)
                dve.wait_ge(max_split, m * 4 + 1)
                nc.vector.tensor_tensor(max_rest[:, :], t, max_parts[:, 0, :], ALU.subtract).then_inc(max_split, 1)
                dve.wait_ge(max_split, m * 4 + 2)
                nc.vector.tensor_copy(max_parts[:, 1, :], max_rest[:, :]).then_inc(max_split, 1)
                dve.wait_ge(max_split, m * 4 + 3)
                nc.vector.tensor_tensor(max_parts[:, 2, :], max_rest[:, :], max_parts[:, 1, :],
                                        ALU.subtract).then_inc(max_split, 1)

            def outputs(n, hf):
                dve.wait_ge(pv_ps, n * NW + (4 * hf + 4 + PV))
                t = o_tok[:, hf, :, :]
                nc.vector.transpose(t.rearrange("p g c -> p (g c)"), bank[6 + hf][:, :]).then_inc(o_turned, 1)
                dve.wait_ge(o_turned, n * 2 + (hf + 1 + OT))
                nc.vector.reciprocal(o_rden[:, hf, :], t.rearrange("p g (b n d) -> p (g b) n d", b=2, n=2)[:, :, 1, 0]
                                     ).then_inc(o_recip, 1)
                dve.wait_ge(o_recip, n * 2 + (hf + 1))
                for p in range(PAIRS):
                    last = nc.vector.tensor_tensor(
                        o_norm[:, hf, :, p * 16:p * 16 + 16].rearrange("p g (b d) -> p g b d", b=2),
                        t[:, p * 8:p * 8 + 8, :].rearrange("p g (b n d) -> p g b n d", b=2, n=2)[:, :, :, 0, :],
                        o_rden[:, hf, p * 16:p * 16 + 16].rearrange("p (g b) -> p g b", b=2).unsqueeze(3)
                        .to_broadcast([P, 8, 2, D]), ALU.mult)
                last.then_inc(o_normed, 1)
                dve.wait_ge(o_normed, n * 2 + (hf + 1))
                dve.wait_ge(proj_ps, n + ONE)
                nc.vector.transpose(o_chan[:, hf * 256:hf * 256 + 256],
                                    o_norm[:, hf, :, :].rearrange("p g c -> p (g c)")).then_inc(o_back, 1)

            def residual(n):
                dve.wait_ge(proj_ps, n + 1 + ONE)
                at = bass.ds(n * CHUNK, CHUNK)
                nc.vector.scalar_tensor_tensor(out=act_all[:, at], in0=bank[0][:, :], scalar=proj_bias[:, 0:1],
                                               in1=x_win[:, at], op0=ALU.add, op1=ALU.add).then_inc(x2_done, 1)

            def both(m, u, n):
                keys(m)
                masks(m, u)
                outputs(n, 0)
                maxima(m)
                split_max(m)
                outputs(n, 1)
                residual(n)

            keys(0)
            masks(0, 0)
            maxima(0)
            split_max(0, first=True)
            with dve.Fori(0, CHUNKS // 2 - 1) as i:
                both(i * 2 + 1, 1, i * 2)
                both(i * 2 + 2, 0, i * 2 + 1)
            both(CHUNKS - 1, 1, CHUNKS - 2)
            outputs(CHUNKS - 1, 0)
            outputs(CHUNKS - 1, 1)
            residual(CHUNKS - 1)

            def wide(k):
                return small[:, k, :].unsqueeze(2).to_broadcast([P, CHUNK // E, E])

            def g(t):
                return t.rearrange("p (g e) -> p g e", e=E)

            with dve.Fori(0, QUADS // 2) as i:
                for u in range(2):
                    quad = i * 2 + u
                    norm_dve(dve, ln2, quad, u, lambda c, j: t_norm[:, u, j, :])
                    steps = [0]

                    def link(ins):
                        steps[0] += 1
                        ins.then_inc(gate_step, 1)
                        dve.wait_ge(gate_step, quad * GATE_OPS + (steps[0] + ONE))

                    v = nc.vector
                    rank8 = const["c_rank"][:, :].unsqueeze(1).to_broadcast([P, CHUNK // E, E])
                    dve.wait_ge(logits_ps, quad + 1)
                    link(v.tensor_scalar(logit, bank[2][:, :], const["c_rb"][:, 0:1], None, ALU.add))
                    link(v.transpose(logit_t, logit))
                    link(v.tensor_reduce(small[:, 0, :], g(logit_t), AX.X, ALU.max))
                    link(v.tensor_tensor(g(g_a), g(logit_t), wide(0), ALU.is_equal))
                    link(v.tensor_tensor(g(g_b), g(g_a), rank8, ALU.mult))
                    link(v.tensor_reduce(small[:, 1, :], g(g_b), AX.X, ALU.max))
                    link(v.tensor_tensor(g(g_mask1), g(g_b), wide(1), ALU.is_equal))
                    link(v.scalar_tensor_tensor(out=g_rest, in0=g_mask1, scalar=FAR, in1=logit_t,
                                                op0=ALU.mult, op1=ALU.add))
                    link(v.tensor_reduce(small[:, 2, :], g(g_rest), AX.X, ALU.max))
                    link(v.tensor_tensor(g(g_a), g(g_rest), wide(2), ALU.is_equal))
                    link(v.tensor_tensor(g(g_b), g(g_a), rank8, ALU.mult))
                    link(v.tensor_reduce(small[:, 3, :], g(g_b), AX.X, ALU.max))
                    link(v.tensor_tensor(g(g_mask2), g(g_b), wide(3), ALU.is_equal))
                    v.tensor_tensor(g(g_diff), g(logit_t), wide(0), ALU.subtract).then_inc(gate_diff, 1)
                    link(v.tensor_tensor(g_a, g_mask1, g_mask2, ALU.add))
                    dve.wait_ge(gate_exp, quad + 1)
                    link(v.tensor_tensor(g_b, g_exp, g_a, ALU.mult))
                    link(v.tensor_reduce(small[:, 4, :], g(g_b), AX.X, ALU.add))
                    link(v.reciprocal(small[:, 5, :], small[:, 4, :]))
                    link(v.tensor_tensor(g(gate_t), g(g_b), wide(5), ALU.mult))
                    dve.wait_ge(y_step, quad * (8 * QUAD) + Y)
                    link(v.transpose(gate_f32, gate_t))
                    v.tensor_copy(gate_parts[:, 0, :], gate_f32).then_inc(gate_part, 1)
                    dve.wait_ge(gate_part, quad * 3 + 1)
                    v.tensor_tensor(g_a, gate_f32, gate_parts[:, 0, :], ALU.subtract).then_inc(gate_part, 1)
                    dve.wait_ge(gate_part, quad * 3 + 2)
                    v.tensor_copy(gate_parts[:, 1, :], g_a).then_inc(gate_part, 1)
                    dve.wait_ge(gate_part, quad * 3 + 3)
                    link(v.tensor_tensor(gate_parts[:, 2, :], g_a, gate_parts[:, 1, :], ALU.subtract))
                    assert steps[0] == GATE_OPS, steps

                    for j in range(QUAD):
                        c = quad * QUAD + j
                        dve.wait_ge(x_rep_in[j % 2], (quad * 2 + (j // 2 + 1)) * (IMG * IMG * 16))
                        for k in range(2 * IMG):
                            dve.wait_ge(gate_ps, c * 8 + (k + 1))
                            dve.wait_ge(y_step, c * 8 + (k + 1))
                            v.tensor_tensor(scaled[:, k % 2, :], x_rep[:, j % 2, k // 2, :], bank[4 + k % 2][:, :],
                                            ALU.mult).then_inc(scaled_done, 1)
                        dve.wait_ge(y_step, c * 8 + (8 + Y))
                        dve.wait_ge(out_free, c + 1)
                        v.tensor_tensor(
                            out_sb[:, j % 2, :].rearrange("p (y win x) -> p win y x", win=NW, y=WS),
                            bank[6 + j % 2][:, :].rearrange("p (win y x) -> p win y x", win=NW, y=WS),
                            act_all[:, bass.ds(c * CHUNK, CHUNK)].rearrange("p (win y x) -> p win y x", win=NW, y=WS),
                            ALU.add).then_inc(summed, 1)


def _layout(i):
    import numpy as np

    f = np.float32
    eye = np.eye(IMG, dtype=f)
    w = {k[len("L0_"):]: np.asarray(v) for k, v in i.items() if k != "x"}
    qkv = w["conv_qkv_w"].reshape(3, C, C)
    qkv_b = w["conv_qkv_b"].reshape(3, C)

    def per_image(block):
        out = np.zeros((IMG, block.shape[0], IMG, block.shape[1]), f)
        for b in range(IMG):
            out[b, :, b, :] = block
        return out.reshape(IMG * block.shape[0], IMG * block.shape[1])

    def column(v):
        return np.tile(v, IMG).reshape(P, 1)

    wv = np.zeros((IMG, C, 2, PAIRS, C), f)
    wp = np.zeros((HEADS, IMG, D, IMG, C), f)
    vb = np.zeros((HEADS, IMG, D, 1), f)
    for b in range(IMG):
        wv[b, :, b % 2, b // 2, :] = qkv[2].T
        wp[:, b, :, b, :] = w["conv_proj_w"].T.reshape(HEADS, D, C)
        vb[:, b, :, 0] = qkv_b[2].reshape(HEADS, D)
    eb = np.zeros((QUAD, IMG, E, QUAD, IMG, C), f)
    for j in range(QUAD):
        for b in range(IMG):
            eb[j, b, :, j, b, :] = w["ffn_expert_b"]
    spread = np.zeros((QUAD, IMG, E, QUAD, IMG, C), f)
    gate = np.zeros((QUAD, IMG, E, IMG, 2, IMG, C), f)
    for b in range(IMG):
        for j in range(QUAD):
            spread[j, b, 0, j, b, :] = 1
        for e in range(E):
            gate[:SPLITS, b, e, b, e // 4, e % 4, :] = 1
    ones = np.zeros((P, 2, TOK), f)
    for b in range(2):
        ones[b * SPLITS:(b + 1) * SPLITS, b, :] = 1
    masks = np.zeros((IMG, HEADS, D, IMG + HEADS), f)
    for b in range(4):
        masks[b, :, :, b] = 1
        masks[:, b, :, IMG + b] = 1
    c = {
        "c_centre": per_image(np.eye(C, dtype=f) - f(1 / C)),
        "c_mean": np.repeat(per_image(np.full((C, 1), 1 / C, f)), E, axis=1),
        "c_spread": spread.reshape(P, QUAD, P),
        "c_eps": np.tile(np.array([EPS_CONV, EPS_FFN, EPS_INST], f), (P, 1)),
        "c_ident": np.eye(P, dtype=f),
        "c_wq": per_image(qkv[0].T), "c_wk": per_image(qkv[1].T), "c_wv": wv.reshape(P, 2, PAIRS * C),
        "c_qb": column(qkv_b[0]), "c_kb": column(qkv_b[1]), "c_vb": vb.reshape(P, 1),
        "c_wp": wp.reshape(P, P), "c_pb": column(w["conv_proj_b"]),
        "c_nw": column(w["conv_norm_w"]), "c_nb": column(w["conv_norm_b"]),
        "c_masks": masks.reshape(P, IMG + HEADS),
        "s_ones": ones.reshape(P, P),
        "c_router": per_image(w["ffn_router_w"]), "c_rb": np.tile(w["ffn_router_b"], P // E).reshape(P, 1),
        "c_rank": np.tile(np.arange(E, 0, -1, dtype=f), (P, 1)),
        "s_gate": gate.reshape(P, 2 * IMG * P),
        "c_we": w["ffn_expert_w"].reshape(2, P, C).transpose(1, 0, 2),
        "c_eb": eb.reshape(P, QUAD, P),
    }
    return {"x": np.asarray(i["x"]), **c}


def kernel(**inputs):
    import numpy as _np
    import concourse.bacc as _bacc
    from concourse import mybir as _mybir
    from concourse.bass_utils import run_bass_kernel_spmd as _run

    nc = _bacc.Bacc("TRN2", target_bir_lowering=False, num_devices=1)
    arrays = {n: _np.ascontiguousarray(a) for n, a in _layout(inputs).items()}
    io = {n: nc.dram_tensor(n if n != "x" else "in_x", a.shape, _mybir.dt.from_np(a.dtype), kind="ExternalInput").ap()
          for n, a in arrays.items()}
    io["out"] = nc.dram_tensor("out_0", (B, C, H, W), _mybir.dt.float32, kind="ExternalOutput").ap()
    metaformer_block(nc, io)
    r = _run(nc, [{(n if n != "x" else "in_x"): a for n, a in arrays.items()}], core_ids=[0])
    return r.results[0]["out_0"]
```

```python
from contextlib import ExitStack

import concourse.bass as bass
from concourse import mybir

B, C, H, W = 8, 32, 64, 64
HEADS, WS, E = 4, 8, 8
D = C // HEADS
TOK = WS * WS
NW = W // WS
P = 128
IMG = P // C
GROUPS = B // IMG
CHUNK = WS * W
BANDS = H // WS
CHUNKS = GROUPS * BANDS
QUAD = 4
QUADS = CHUNKS // QUAD
PAIRS = IMG // 2
HALVES = HEADS // 2
SPLITS = 3
SCALE = float(D) ** -0.5
EPS_CONV, EPS_FFN, EPS_INST = 1e-6, 1e-5, 1e-6
FAR = -3.0e38

F32 = mybir.dt.float32
BF16 = mybir.dt.bfloat16
ALU = mybir.AluOpType
ACT = mybir.ActivationFunctionType
AX = mybir.AxisListType


def metaformer_block(nc, io):
    x_v = io["x"].rearrange("(g b) c y x -> g (b c) (y x)", b=IMG)
    out_v = io["out"].rearrange("(g b) c (n y) x -> (b c) g n (y x)", b=IMG, y=WS)

    with ExitStack() as ctx:
        def sb(name, shape, dt=F32):
            return ctx.enter_context(nc.sbuf_tensor(name, shape, dt))

        def sem(name):
            return ctx.enter_context(nc.semaphore(name))

        stage = sb("stage", [P, CHUNKS * CHUNK])
        x_win = sb("x_win", [P, CHUNKS * CHUNK])
        act_all = sb("act_all", [P, CHUNKS * CHUNK])
        half = 2 * IMG * CHUNK
        q_img = stage[:, 0:half].rearrange("p (u win b t) -> p u win b t", u=2, win=NW, b=IMG)
        k_head = stage[:, half:2 * half].rearrange("p (u h n) -> p u h n", u=2, h=HEADS)
        x_rep = stage[:, 0:half].rearrange("p (u b n) -> p u b n", u=2, b=IMG)
        t_norm = stage[:, half:2 * half].rearrange("p (u j n) -> p u j n", u=2, j=QUAD)
        work = sb("work", [P, 2 * IMG * CHUNK])
        centred = work[:, :].rearrange("p (u j n) -> p u j n", u=2, j=QUAD)
        shifted = work[:, 0:4 * CHUNK].rearrange("p (s n) -> p s n", s=4)
        v_cols = sb("v_cols", [P, 2, NW * IMG * HALVES, 2, 2, D])
        v_flat = v_cols[:].rearrange("p u g b n d -> p (u g b n d)")
        late = sb("late", [P, QUAD * CHUNK])
        squares = late[:, :].rearrange("p (j n) -> p j n", j=QUAD)
        std = sb("std", [P, CHUNK])
        rstd = sb("rstd", [P, CHUNK])
        stats = sb("stats", [P, CHUNKS, 6])
        moments = sb("moments", [P, GROUPS, 2])
        inst = sb("inst", [P, 4, GROUPS])
        inst_s = sb("inst_s", [P, CHUNKS])
        inst_t = sb("inst_t", [P, CHUNKS])
        x_cur = sb("x_cur", [P, 2, CHUNK])
        q_sb = sb("q_sb", [P, CHUNK])
        k_sb = sb("k_sb", [P, CHUNK])
        neg_max = sb("neg_max", [P, 4, PAIRS * HEADS])
        rows = sb("rows", [P, 7 * CHUNK])
        probs = late[:, :].rearrange("p (s n) -> p s n", s=4)
        o_tok = sb("o_tok", [P, 2, 16, 32])
        o_rden = sb("o_rden", [P, 2, 32])
        o_norm = sb("o_norm", [P, 2, 8, 32])
        o_chan = sb("o_chan", [P, CHUNK])
        gate_parts = sb("gate_parts", [P, SPLITS, CHUNK], BF16)
        gate_rows = sb("gate_rows", [P, QUAD, CHUNK], BF16)
        scaled = rows[:, 0:2 * CHUNK].rearrange("p (u n) -> p u n", u=2)
        out_sb = rows[:, 2 * CHUNK:4 * CHUNK].rearrange("p (u n) -> p u n", u=2)

        def g3(k):
            return v_flat[:, k * CHUNK:(k + 1) * CHUNK].rearrange("p (g e) -> p g e", e=E)

        logit, logit_t, g_a, g_b, g_mask1, g_mask2, g_rest, gate_t = (
            v_flat[:, k * CHUNK:(k + 1) * CHUNK] for k in range(8))
        small = sb("small", [P, 6, CHUNK // E])
        g_diff, g_exp, gate_f32 = (rows[:, k * CHUNK:(k + 1) * CHUNK] for k in range(4, 7))

        const = {n: sb("sb_" + n, list(a.shape)) for n, a in io.items() if n.startswith("c_")}
        gate_in = x_cur[:, :, :].rearrange("p u n -> p (u n)")
        gate_sel = sb("gate_sel", [P, 2 * IMG * P], BF16)
        qb_scaled = sb("qb_scaled", [P, 1])
        proj_bias = sb("proj_bias", [P, 1])

        bank = [ctx.enter_context(nc.psum_tensor(f"bank{i}", [P, 512], F32)) for i in range(8)]

        x_loaded = [sem(f"x_loaded{g}") for g in range(GROUPS)]
        consts_loaded = sem("consts_loaded")
        filled = sem("filled")
        x_win_ready = sem("x_win_ready")

        def norm_sems(tag):
            return {n: sem(f"{tag}_{n}") for n in
                    ("centred_ps", "squared", "var_ps", "std_ready", "rstd_ready", "rstd_ps", "normed")}

        ln1, ln2 = norm_sems("ln1"), norm_sems("ln2")
        stats_done = sem("stats_done")
        inst_step = sem("inst_step")
        inst_std = sem("inst_std")
        affine_ready = sem("affine_ready")
        bias_ps = sem("bias_ps")
        biases_ready = sem("biases_ready")
        x_cur_ready = sem("x_cur_ready")
        q_ps = sem("q_ps")
        k_ps = sem("k_ps")
        v_ps = sem("v_ps")
        q_done = sem("q_done")
        k_done = sem("k_done")
        v_done = sem("v_done")
        q_masks = sem("q_masks")
        k_masks = sem("k_masks")
        score_ps = sem("score_ps")
        max_done = sem("max_done")
        shifted_done = sem("shifted_done")
        turned_ps = sem("turned_ps")
        exp_done = sem("exp_done")
        pv_ps = sem("pv_ps")
        o_turned = sem("o_turned")
        o_recip = sem("o_recip")
        o_normed = sem("o_normed")
        o_back = sem("o_back")
        proj_ps = sem("proj_ps")
        x2_done = sem("x2_done")
        logits_ps = sem("logits_ps")
        gate_step = sem("gate_step")
        gate_diff = sem("gate_diff")
        gate_part = sem("gate_part")
        gate_exp = sem("gate_exp")
        gates_in = sem("gates_in")
        x_rep_in = [sem(f"x_rep_in{u}") for u in range(2)]
        gate_ps = sem("gate_ps")
        scaled_done = sem("scaled_done")
        y_step = sem("y_step")
        summed = sem("summed")
        stored = sem("stored")
        out_free = sem("out_free")

        XC, NORMED, X2, SH, EXP, OT, SC, Y, SUM, OUT, ONE = 2, 8, 3, 2, 2, 2, 2, 2, 2, 2, 1
        GATE_OPS = 20

        block = ctx.enter_context(nc.Block())

        @block.sync
        def _(sp):
            for g in range(GROUPS):
                sp.dma_start(stage[:, g * BANDS * CHUNK:(g + 1) * BANDS * CHUNK], x_v[g]).then_inc(x_loaded[g], 16)

            with sp.Fori(0, QUADS // 2) as i:
                for u in range(2):
                    quad = i * 2 + u
                    split_all, used = sp.snap(quad * GATE_OPS + (GATE_OPS + ONE)), sp.snap(quad * (8 * QUAD) + Y)
                    done = [sp.snap(quad * QUAD + (j + 1)) for j in range(QUAD)]
                    sp.wait_ge(gate_step, split_all)
                    sp.wait_ge(y_step, used)
                    for j in range(QUAD):
                        for s in range(SPLITS):
                            sp.dma_start(gate_rows[32 * s:32 * s + 32, j, :],
                                         gate_parts[32 * j:32 * j + 32, s, :]).then_inc(gates_in, 16)
                    for j in range(QUAD):
                        sp.wait_ge(summed, done[j])
                        for b in range(IMG):
                            for e in range(IMG):
                                sp.dma_start(x_rep[32 * e:32 * e + 32, j % 2, b, :],
                                             t_norm[32 * b:32 * b + 32, u, j, :]).then_inc(x_rep_in[j % 2], 16)

        @block.gpsimd
        def _(pool):
            pool.sem_inc(out_free, OUT)
            for n in const:
                pool.dma_start(const[n][:], io[n]).then_inc(consts_loaded, 16)
            pool.dma_start(gate_in, io["s_gate"]).then_inc(consts_loaded, 16)
            pool.memset(v_flat, 0.0).then_inc(filled, 1)
            pool.memset(gate_rows[:, :, :], 0.0).then_inc(filled, 1)
            pool.wait_ge(filled, 2)
            for b in range(2):
                pool.memset(v_cols[b * 64:b * 64 + 64, :, :, b, 1, :].rearrange("p u g d -> p (u g) d"),
                            1.0).then_inc(filled, 1)
                pool.wait_ge(filled, 3 + b)
            for g in range(GROUPS):
                pool.wait_ge(x_loaded[g], 16)
                with pool.Fori(g * BANDS, (g + 1) * BANDS) as c:
                    pool.tensor_copy(
                        x_win[:, bass.ds(c * CHUNK, CHUNK)].rearrange("p (win y x) -> p win y x", win=NW, y=WS),
                        stage[:, bass.ds(c * CHUNK, CHUNK)].rearrange("p (y win x) -> p win y x", win=NW, y=WS),
                    ).then_inc(x_win_ready, 1)
            with pool.Fori(0, QUADS // 2) as i:
                for u in range(2):
                    for j in range(QUAD):
                        c = i * (2 * QUAD) + (u * QUAD + j)
                        pool.wait_ge(summed, c + 1 + SUM)
                        pool.dma_start(out_v[:, bass.ds(i, 1), u * QUAD + j, :].rearrange("p a n -> p (a n)"),
                                       out_sb[:, j % 2, :]).then_inc(stored, 16)
                        pool.wait_ge(stored, c * 16 + 16)
                        pool.sem_inc(out_free, 1)

        def norm_pe(pe, sems, quad, u, source, first_wait, bank2_free):
            for j in range(QUAD):
                c = quad * QUAD + j
                first_wait(c)
                pe.wait_ge(sems["squared"], c + 1)
                nc.tensor.matmul(bank[j % 2][:, :], const["c_centre"][:, :], source[:, bass.ds(c * CHUNK, CHUNK)],
                                 start=True, stop=True).then_inc(sems["centred_ps"], 1)
            for j in range(QUAD):
                if j == 0:
                    pe.wait_ge(sems["std_ready"], quad + ONE)
                    bank2_free()
                pe.wait_ge(sems["squared"], quad * QUAD + j + 1 + XC)
                last = nc.tensor.matmul(bank[2][32 * j:32 * j + 32, :], const["c_mean"][:, :], squares[:, j, :],
                                        start=True, stop=True)
            last.then_inc(sems["var_ps"], 1)
            for j in range(QUAD):
                if j == 0:
                    pe.wait_ge(sems["rstd_ready"], quad + 1 + ONE)
                pe.wait_ge(sems["normed"], quad * QUAD + j + NORMED)
                nc.tensor.matmul(bank[3][:, :], const["c_spread"][:, j, :], rstd[:, :],
                                 start=True, stop=True).then_inc(sems["rstd_ps"], 1)

        def norm_act(act, sems, quad, u, eps):
            for j in range(QUAD):
                c = quad * QUAD + j
                act.wait_ge(sems["centred_ps"], c + 1)
                act.wait_ge(sems["normed"], c + 1)
                nc.scalar.activation(centred[:, u, j, :], bank[j % 2][:, :], ACT.Copy)
                act.wait_ge(sems["var_ps"], quad + ONE)
                nc.scalar.activation(squares[:, j, :], bank[j % 2][:, :], ACT.Square).then_inc(sems["squared"], 1)
            act.wait_ge(sems["var_ps"], quad + 1 + ONE)
            act.wait_ge(sems["rstd_ready"], quad + ONE)
            nc.scalar.activation(std[:, :], bank[2][:, :], ACT.Sqrt, bias=eps).then_inc(sems["std_ready"], 1)

        def norm_dve(dve, sems, quad, u, target):
            dve.wait_ge(sems["std_ready"], quad + 1 + ONE)
            dve.wait_ge(sems["rstd_ps"], quad * QUAD + ONE)
            nc.vector.reciprocal(rstd[:, :], std[:, :]).then_inc(sems["rstd_ready"], 1)
            for j in range(QUAD):
                c = quad * QUAD + j
                dve.wait_ge(sems["rstd_ps"], c + 1 + ONE)
                dve.wait_ge(sems["squared"], c + 1 + XC)
                nc.vector.tensor_tensor(target(c, j), centred[:, u, j, :], bank[3][:, :],
                                        ALU.mult).then_inc(sems["normed"], 1)

        @block.tensor
        def _(pe):
            for s, k in ((proj_ps, ONE), (ln1["var_ps"], ONE), (ln2["var_ps"], ONE),
                         (ln1["rstd_ps"], ONE), (ln2["rstd_ps"], ONE)):
                pe.sem_inc(s, k)
            pe.sem_inc(y_step, Y)
            pe.wait_ge(consts_loaded, 16 * (len(const) + 1))
            nc.tensor.matmul(bank[7][:, 0:1], const["c_wp"][:, :], const["c_vb"][:, :],
                             start=True, stop=True).then_inc(bias_ps, 1)
            with pe.Fori(0, QUADS // 2) as i:
                for u in range(2):
                    norm_pe(pe, ln1, i * 2 + u, u, x_win,
                            lambda c: pe.wait_ge(x_win_ready, c + 1), lambda: None)

            def queries(m):
                pe.wait_ge(x_cur_ready, m + 1)
                pe.wait_ge(x2_done, m + 1)
                nc.tensor.matmul(bank[0][:, :], const["c_wq"][:, :], x_cur[:, 0, :],
                                 start=True, stop=True).then_inc(q_ps, 1)

            def keys(m):
                pe.wait_ge(q_done, m + 1)
                nc.tensor.matmul(bank[0][:, :], const["c_wk"][:, :], x_cur[:, 0, :],
                                 start=True, stop=True).then_inc(k_ps, 1)

            def values(m):
                pe.wait_ge(v_done, m * 2)
                for w in range(NW):
                    for hl in range(2):
                        last = nc.tensor.matmul(bank[1][64 * hl:64 * hl + 64, w * 64:w * 64 + 64],
                                                x_cur[:, 0, w * TOK:w * TOK + TOK], const["c_wv"][:, hl, :],
                                                start=True, stop=True)
                last.then_inc(v_ps, 1)

            def score(m, u, w):
                if w == 0:
                    pe.wait_ge(q_masks, m + 1)
                    pe.wait_ge(k_masks, m + 1)
                pe.wait_ge(shifted_done, m * NW + (w + 1))
                for p in range(PAIRS):
                    last = nc.tensor.matmul(bank[2 + w % 2][:, p * 256:p * 256 + 256],
                                            q_img[:, u, w, 2 * p:2 * p + 2, :].rearrange("p b t -> p (b t)"),
                                            k_head[:, u, :, w * TOK:w * TOK + TOK], start=True, stop=True)
                last.then_inc(score_ps, 1)

            def turn(n, w):
                pe.wait_ge(shifted_done, n * NW + (w + 1 + SH))
                pe.wait_ge(exp_done, n * NW + (w + 1))
                for k in range(PAIRS * HALVES):
                    last = nc.tensor.transpose(bank[4 + w % 2][:, k * P:k * P + P],
                                               shifted[:, w % 4, k * P:k * P + P], const["c_ident"][:, :])
                last.then_inc(turned_ps, 1)

            def weigh(n, u, w):
                if w == 0:
                    pe.wait_ge(v_done, n * 2 + 2)
                if w % 4 == 0:
                    pe.wait_ge(o_turned, n * 2 + (w // 4 + 1))
                pe.wait_ge(exp_done, n * NW + (w + 1 + EXP))
                for b in range(IMG):
                    for hh in range(HALVES):
                        at, k = hh * 256 + (w % 4) * TOK, (b // 2) * HALVES + hh
                        last = nc.tensor.matmul(
                            bank[6 + w // 4][32 * b:32 * b + 32, at:at + TOK],
                            v_cols[:, u, (w * IMG + b) * HALVES + hh, :, :, :].rearrange("p b n d -> p (b n d)"),
                            probs[:, w % 4, k * P + (b % 2) * TOK:k * P + (b % 2) * TOK + TOK],
                            start=True, stop=True)
                last.then_inc(pv_ps, 1)

            def project(n, k_waits):
                pe.wait_ge(o_back, n * 2 + 2)
                pe.wait_ge(k_done, k_waits)
                nc.tensor.matmul(bank[0][:, :], const["c_wp"][:, :], o_chan[:, :],
                                 start=True, stop=True).then_inc(proj_ps, 1)

            def chunk(m, u, first=False, final=False):
                for w in range(NW):
                    score(m, u, w)
                    if not final:
                        if w == 1:
                            queries(m + 1)
                        if w == 2:
                            keys(m + 1)
                    if w >= 2:
                        turn(m, w - 2)
                    elif not first:
                        turn(m - 1, w - 2 + NW)
                    if w >= 3:
                        weigh(m, u, w - 3)
                    elif not first:
                        weigh(m - 1, 1 - u, w - 3 + NW)
                    if w == 4 and not final:
                        values(m + 1)
                    if w == 6 and not first:
                        project(m - 1, CHUNKS if final else m + 2)

            pe.wait_ge(biases_ready, 1)
            queries(0)
            keys(0)
            values(0)
            chunk(0, 0, first=True)
            with pe.Fori(0, CHUNKS // 2 - 1) as i:
                chunk(i * 2 + 1, 1)
                chunk(i * 2 + 2, 0)
            chunk(CHUNKS - 1, 1, final=True)
            turn(CHUNKS - 1, NW - 2)
            weigh(CHUNKS - 1, 1, NW - 3)
            turn(CHUNKS - 1, NW - 1)
            weigh(CHUNKS - 1, 1, NW - 2)
            weigh(CHUNKS - 1, 1, NW - 1)
            project(CHUNKS - 1, CHUNKS)

            pe.wait_ge(x2_done, CHUNKS + X2)
            with pe.Fori(0, QUADS // 2) as i:
                for u in range(2):
                    quad = i * 2 + u
                    norm_pe(pe, ln2, quad, u, act_all, lambda c: None,
                            lambda: pe.wait_ge(gate_step, quad * GATE_OPS + ONE))
                    for j in range(QUAD):
                        c = quad * QUAD + j
                        pe.wait_ge(ln2["normed"], c + 1 + NORMED)
                        if j == 0:
                            pe.wait_ge(ln2["std_ready"], quad + 1 + ONE)
                        last = nc.tensor.matmul(bank[2][32 * j:32 * j + 32, :], const["c_router"][:, :],
                                                t_norm[:, u, j, :], start=True, stop=True)
                    last.then_inc(logits_ps, 1)
                    pe.wait_ge(gates_in, quad * (QUAD * SPLITS * 16) + QUAD * SPLITS * 16)
                    for j in range(QUAD):
                        c = quad * QUAD + j
                        y = bank[6 + j % 2]
                        pe.wait_ge(summed, c + 1)
                        nc.tensor.matmul(y[:, :], const["c_eb"][:, j, :], gate_f32,
                                         start=True, stop=False, skip_group_check=True)

                        def spread(k):
                            pe.wait_ge(scaled_done, c * 8 + (k + 1))
                            nc.tensor.matmul(bank[4 + k % 2][:, :], gate_sel[:, k * P:(k + 1) * P], gate_rows[:, j, :],
                                             start=True, stop=True).then_inc(gate_ps, 1)

                        def expert(k):
                            b, eh = k // 2, k % 2
                            pe.wait_ge(scaled_done, c * 8 + (k + 1 + SC))
                            mm = nc.tensor.matmul(y[32 * b:32 * b + 32, :], const["c_we"][:, eh, :],
                                                  scaled[:, k % 2, :], start=False, stop=(eh == 1),
                                                  skip_group_check=True)
                            mm.then_inc(y_step, 1)
                            return mm

                        spread(0)
                        for k in range(1, 2 * IMG):
                            spread(k)
                            expert(k - 1)
                        expert(2 * IMG - 1)

        @block.scalar
        def _(act):
            for sems in (ln1, ln2):
                act.sem_inc(sems["squared"], XC)
                act.sem_inc(sems["std_ready"], ONE)
            act.sem_inc(exp_done, EXP)
            with act.Fori(0, QUADS // 2) as i:
                for u in range(2):
                    norm_act(act, ln1, i * 2 + u, u, const["c_eps"][:, 0:1])
            act.wait_ge(inst_step, 2)
            nc.scalar.activation(inst[:, 0, :], moments[:, :, 1], ACT.Sqrt, bias=const["c_eps"][:, 2:3]
                                 ).then_inc(inst_std, 1)

            def current(m):
                nc.scalar.activation(x_cur[:, 0, :], act_all[:, bass.ds(m * CHUNK, CHUNK)], ACT.Identity,
                                     bias=inst_t[:, bass.ds(m, 1)], scale=inst_s[:, bass.ds(m, 1)]
                                     ).then_inc(x_cur_ready, 1)

            def copy_queries(m):
                act.wait_ge(q_ps, m + 1)
                act.wait_ge(q_masks, m)
                nc.scalar.activation(q_sb[:, :], bank[0][:, :], ACT.Identity, bias=qb_scaled[:, 0:1],
                                     scale=SCALE).then_inc(q_done, 1)

            def copy_keys(m):
                act.wait_ge(k_ps, m + 1)
                act.wait_ge(k_masks, m)
                nc.scalar.activation(k_sb[:, :], bank[0][:, :], ACT.Identity,
                                     bias=const["c_kb"][:, 0:1]).then_inc(k_done, 1)

            def mask_keys(m, u, h):
                if h == 0:
                    act.wait_ge(k_done, m + 1)
                one = nc.scalar.activation(k_head[:, u, h, :], k_sb[:, :], ACT.Copy,
                                           scale=const["c_masks"][:, IMG + h:IMG + h + 1])
                if h == HEADS - 1:
                    one.then_inc(k_masks, 1)

            def copy_values(m, u):
                act.wait_ge(v_ps, m + 1)
                for hl in range(2):
                    nc.scalar.activation(v_cols[64 * hl:64 * hl + 64, u, :, hl, 0, :],
                                         bank[1][64 * hl:64 * hl + 64, :].rearrange("p (g d) -> p g d", d=D),
                                         ACT.Copy).then_inc(v_done, 1)

            def exps(n, w):
                act.wait_ge(turned_ps, n * NW + (w + 1))
                nc.scalar.activation(probs[:, w % 4, :], bank[4 + w % 2][:, :], ACT.Exp).then_inc(exp_done, 1)

            def chunk(m, u, first=False, final=False):
                for w in range(NW):
                    if w >= 2:
                        exps(m, w - 2)
                    elif not first:
                        exps(m - 1, w - 2 + NW)
                    if not final:
                        if w == 0:
                            current(m + 1)
                        if w == 1:
                            copy_queries(m + 1)
                        if w == 2:
                            copy_keys(m + 1)
                        if 3 <= w < 3 + HEADS:
                            mask_keys(m + 1, 1 - u, w - 3)
                        if w == 5:
                            copy_values(m + 1, 1 - u)

            act.wait_ge(affine_ready, 1)
            current(0)
            copy_queries(0)
            copy_keys(0)
            for h in range(HEADS):
                mask_keys(0, 0, h)
            act.wait_ge(filled, 4)
            copy_values(0, 0)
            chunk(0, 0, first=True)
            with act.Fori(0, CHUNKS // 2 - 1) as i:
                chunk(i * 2 + 1, 1)
                chunk(i * 2 + 2, 0)
            chunk(CHUNKS - 1, 1, final=True)
            exps(CHUNKS - 1, NW - 2)
            exps(CHUNKS - 1, NW - 1)

            with act.Fori(0, QUADS // 2) as i:
                for u in range(2):
                    quad = i * 2 + u
                    norm_act(act, ln2, quad, u, const["c_eps"][:, 1:2])
                    act.wait_ge(gate_diff, quad + 1)
                    nc.scalar.activation(g_exp, g_diff, ACT.Exp).then_inc(gate_exp, 1)

        @block.vector
        def _(dve):
            for s, k in ((ln1["normed"], NORMED), (ln2["normed"], NORMED), (x2_done, X2), (o_turned, OT),
                         (shifted_done, SH), (scaled_done, SC), (summed, SUM), (gate_step, ONE),
                         (ln1["rstd_ready"], ONE), (ln2["rstd_ready"], ONE)):
                dve.sem_inc(s, k)
            dve.wait_ge(consts_loaded, 16 * (len(const) + 1))
            nc.vector.tensor_scalar(qb_scaled[:, :], const["c_qb"][:, :], SCALE, None, ALU.mult)
            nc.vector.tensor_copy(gate_sel[:, :], gate_in)
            dve.wait_ge(bias_ps, 1)
            nc.vector.tensor_tensor(proj_bias[:, :], bank[7][:, 0:1], const["c_pb"][:, :],
                                    ALU.add).then_inc(biases_ready, 1)
            with dve.Fori(0, QUADS // 2) as i:
                for u in range(2):
                    norm_dve(dve, ln1, i * 2 + u, u, lambda c, j: act_all[:, bass.ds(c * CHUNK, CHUNK)])
                    for j in range(QUAD):
                        c = (i * 2 + u) * QUAD + j
                        dve.wait_ge(ln1["normed"], c + 1 + NORMED)
                        nc.vector.bn_stats(stats[:, bass.ds(c, 1), :].rearrange("p a s -> p (a s)"),
                                           act_all[:, bass.ds(c * CHUNK, CHUNK)]).then_inc(stats_done, 1)
            dve.wait_ge(stats_done, CHUNKS)
            for g in range(GROUPS):
                nc.vector.bn_aggr(moments[:, g, :], stats[:, g * BANDS:(g + 1) * BANDS, :]
                                  .rearrange("p n s -> p (n s)")).then_inc(inst_step, 1)
            dve.wait_ge(inst_std, 1)
            nc.vector.reciprocal(inst[:, 1, :], inst[:, 0, :]).then_inc(inst_step, 1)
            dve.wait_ge(inst_step, 3)
            nc.vector.tensor_scalar(inst[:, 2, :], inst[:, 1, :], const["c_nw"][:, 0:1], None,
                                    ALU.mult).then_inc(inst_step, 1)
            dve.wait_ge(inst_step, 4)
            nc.vector.tensor_tensor(inst[:, 3, :], moments[:, :, 0], inst[:, 2, :], ALU.mult).then_inc(inst_step, 1)
            dve.wait_ge(inst_step, 5)
            for g in range(GROUPS):
                at = slice(g * BANDS, (g + 1) * BANDS)
                nc.vector.tensor_copy(inst_s[:, at], inst[:, 2, g:g + 1].to_broadcast([P, BANDS]))
                last = nc.vector.tensor_scalar(inst_t[:, at], inst[:, 3, g:g + 1].to_broadcast([P, BANDS]),
                                               -1.0, const["c_nb"][:, 0:1], ALU.mult, ALU.add)
            last.then_inc(affine_ready, 1)

            def mask_queries(m, u, b):
                dve.wait_ge(q_done, m + 1)
                one = nc.vector.tensor_scalar(q_img[:, u, :, b, :], q_sb[:, :].rearrange("p (win t) -> p win t", win=NW),
                                              const["c_masks"][:, b:b + 1], None, ALU.mult)
                if b == IMG - 1:
                    one.then_inc(q_masks, 1)

            def shift(m, w):
                dve.wait_ge(score_ps, m * NW + (w + 1))
                t = bank[2 + w % 2][:, :].rearrange("p (g k) -> p g k", k=TOK)
                nc.vector.tensor_reduce(neg_max[:, w % 4, :], t, AX.X, ALU.max, negate=True).then_inc(max_done, 1)
                dve.wait_ge(max_done, m * NW + (w + 1))
                nc.vector.tensor_tensor(shifted[:, w % 4, :].rearrange("p (g k) -> p g k", k=TOK), t,
                                        neg_max[:, w % 4, :].unsqueeze(2).to_broadcast([P, PAIRS * HEADS, TOK]),
                                        ALU.add).then_inc(shifted_done, 1)

            def outputs(n, hf):
                dve.wait_ge(pv_ps, n * NW + (4 * hf + 4))
                t = o_tok[:, hf, :, :]
                nc.vector.transpose(t.rearrange("p g c -> p (g c)"), bank[6 + hf][:, :]).then_inc(o_turned, 1)
                dve.wait_ge(o_turned, n * 2 + (hf + 1 + OT))
                nc.vector.reciprocal(o_rden[:, hf, :], t.rearrange("p g (b n d) -> p (g b) n d", b=2, n=2)[:, :, 1, 0]
                                     ).then_inc(o_recip, 1)
                dve.wait_ge(o_recip, n * 2 + (hf + 1))
                for p in range(PAIRS):
                    last = nc.vector.tensor_tensor(
                        o_norm[:, hf, :, p * 16:p * 16 + 16].rearrange("p g (b d) -> p g b d", b=2),
                        t[:, p * 8:p * 8 + 8, :].rearrange("p g (b n d) -> p g b n d", b=2, n=2)[:, :, :, 0, :],
                        o_rden[:, hf, p * 16:p * 16 + 16].rearrange("p (g b) -> p g b", b=2).unsqueeze(3)
                        .to_broadcast([P, 8, 2, D]), ALU.mult)
                last.then_inc(o_normed, 1)
                dve.wait_ge(o_normed, n * 2 + (hf + 1))
                dve.wait_ge(proj_ps, n + ONE)
                nc.vector.transpose(o_chan[:, hf * 256:hf * 256 + 256],
                                    o_norm[:, hf, :, :].rearrange("p g c -> p (g c)")).then_inc(o_back, 1)

            def residual(n):
                dve.wait_ge(proj_ps, n + 1 + ONE)
                at = bass.ds(n * CHUNK, CHUNK)
                nc.vector.scalar_tensor_tensor(out=act_all[:, at], in0=bank[0][:, :], scalar=proj_bias[:, 0:1],
                                               in1=x_win[:, at], op0=ALU.add, op1=ALU.add).then_inc(x2_done, 1)

            def chunk(m, u, first=False, final=False):
                for w in range(NW):
                    shift(m, w)
                    if 3 <= w < 3 + IMG and not final:
                        mask_queries(m + 1, 1 - u, w - 3)
                    if w == 3 and not first:
                        outputs(m - 1, 1)
                    if w == NW - 1:
                        if not first:
                            residual(m - 1)
                        outputs(m, 0)

            for b in range(IMG):
                mask_queries(0, 0, b)
            chunk(0, 0, first=True)
            with dve.Fori(0, CHUNKS // 2 - 1) as i:
                chunk(i * 2 + 1, 1)
                chunk(i * 2 + 2, 0)
            chunk(CHUNKS - 1, 1, final=True)
            outputs(CHUNKS - 1, 1)
            residual(CHUNKS - 1)

            def wide(k):
                return small[:, k, :].unsqueeze(2).to_broadcast([P, CHUNK // E, E])

            def g(t):
                return t.rearrange("p (g e) -> p g e", e=E)

            with dve.Fori(0, QUADS // 2) as i:
                for u in range(2):
                    quad = i * 2 + u
                    norm_dve(dve, ln2, quad, u, lambda c, j: t_norm[:, u, j, :])
                    steps = [0]

                    def link(ins):
                        steps[0] += 1
                        ins.then_inc(gate_step, 1)
                        dve.wait_ge(gate_step, quad * GATE_OPS + (steps[0] + ONE))

                    v = nc.vector
                    rank8 = const["c_rank"][:, :].unsqueeze(1).to_broadcast([P, CHUNK // E, E])
                    dve.wait_ge(logits_ps, quad + 1)
                    link(v.tensor_scalar(logit, bank[2][:, :], const["c_rb"][:, 0:1], None, ALU.add))
                    link(v.transpose(logit_t, logit))
                    link(v.tensor_reduce(small[:, 0, :], g(logit_t), AX.X, ALU.max))
                    link(v.tensor_tensor(g(g_a), g(logit_t), wide(0), ALU.is_equal))
                    link(v.tensor_tensor(g(g_b), g(g_a), rank8, ALU.mult))
                    link(v.tensor_reduce(small[:, 1, :], g(g_b), AX.X, ALU.max))
                    link(v.tensor_tensor(g(g_mask1), g(g_b), wide(1), ALU.is_equal))
                    link(v.scalar_tensor_tensor(out=g_rest, in0=g_mask1, scalar=FAR, in1=logit_t,
                                                op0=ALU.mult, op1=ALU.add))
                    link(v.tensor_reduce(small[:, 2, :], g(g_rest), AX.X, ALU.max))
                    link(v.tensor_tensor(g(g_a), g(g_rest), wide(2), ALU.is_equal))
                    link(v.tensor_tensor(g(g_b), g(g_a), rank8, ALU.mult))
                    link(v.tensor_reduce(small[:, 3, :], g(g_b), AX.X, ALU.max))
                    link(v.tensor_tensor(g(g_mask2), g(g_b), wide(3), ALU.is_equal))
                    v.tensor_tensor(g(g_diff), g(logit_t), wide(0), ALU.subtract).then_inc(gate_diff, 1)
                    link(v.tensor_tensor(g_a, g_mask1, g_mask2, ALU.add))
                    dve.wait_ge(gate_exp, quad + 1)
                    link(v.tensor_tensor(g_b, g_exp, g_a, ALU.mult))
                    link(v.tensor_reduce(small[:, 4, :], g(g_b), AX.X, ALU.add))
                    link(v.reciprocal(small[:, 5, :], small[:, 4, :]))
                    link(v.tensor_tensor(g(gate_t), g(g_b), wide(5), ALU.mult))
                    dve.wait_ge(y_step, quad * (8 * QUAD) + Y)
                    link(v.transpose(gate_f32, gate_t))
                    v.tensor_copy(gate_parts[:, 0, :], gate_f32).then_inc(gate_part, 1)
                    dve.wait_ge(gate_part, quad * 3 + 1)
                    v.tensor_tensor(g_a, gate_f32, gate_parts[:, 0, :], ALU.subtract).then_inc(gate_part, 1)
                    dve.wait_ge(gate_part, quad * 3 + 2)
                    v.tensor_copy(gate_parts[:, 1, :], g_a).then_inc(gate_part, 1)
                    dve.wait_ge(gate_part, quad * 3 + 3)
                    link(v.tensor_tensor(gate_parts[:, 2, :], g_a, gate_parts[:, 1, :], ALU.subtract))
                    assert steps[0] == GATE_OPS, steps

                    for j in range(QUAD):
                        c = quad * QUAD + j
                        dve.wait_ge(x_rep_in[j % 2], (quad * 2 + (j // 2 + 1)) * (IMG * IMG * 16))
                        for k in range(2 * IMG):
                            dve.wait_ge(gate_ps, c * 8 + (k + 1))
                            dve.wait_ge(y_step, c * 8 + (k + 1))
                            v.tensor_tensor(scaled[:, k % 2, :], x_rep[:, j % 2, k // 2, :], bank[4 + k % 2][:, :],
                                            ALU.mult).then_inc(scaled_done, 1)
                        dve.wait_ge(y_step, c * 8 + (8 + Y))
                        dve.wait_ge(out_free, c + 1)
                        v.tensor_tensor(
                            out_sb[:, j % 2, :].rearrange("p (y win x) -> p win y x", win=NW, y=WS),
                            bank[6 + j % 2][:, :].rearrange("p (win y x) -> p win y x", win=NW, y=WS),
                            act_all[:, bass.ds(c * CHUNK, CHUNK)].rearrange("p (win y x) -> p win y x", win=NW, y=WS),
                            ALU.add).then_inc(summed, 1)


def _layout(i):
    import numpy as np

    f = np.float32
    eye = np.eye(IMG, dtype=f)
    w = {k[len("L0_"):]: np.asarray(v) for k, v in i.items() if k != "x"}
    qkv = w["conv_qkv_w"].reshape(3, C, C)
    qkv_b = w["conv_qkv_b"].reshape(3, C)

    def per_image(block):
        out = np.zeros((IMG, block.shape[0], IMG, block.shape[1]), f)
        for b in range(IMG):
            out[b, :, b, :] = block
        return out.reshape(IMG * block.shape[0], IMG * block.shape[1])

    def column(v):
        return np.tile(v, IMG).reshape(P, 1)

    wv = np.zeros((IMG, C, 2, IMG, HALVES, D), f)
    for b in range(IMG):
        wv[b, :, :, b] = qkv[2].T.reshape(C, HALVES, 2, D).transpose(0, 2, 1, 3)
    eb = np.zeros((QUAD, IMG, E, QUAD, IMG, C), f)
    for j in range(QUAD):
        for b in range(IMG):
            eb[j, b, :, j, b, :] = w["ffn_expert_b"]
    spread = np.zeros((QUAD, IMG, E, QUAD, IMG, C), f)
    gate = np.zeros((QUAD, IMG, E, IMG, 2, IMG, C), f)
    for b in range(IMG):
        for j in range(QUAD):
            spread[j, b, 0, j, b, :] = 1
        for e in range(E):
            gate[:SPLITS, b, e, b, e // 4, e % 4, :] = 1
    masks = np.zeros((IMG, HEADS, D, IMG + HEADS), f)
    for b in range(4):
        masks[b, :, :, b] = 1
        masks[:, b, :, IMG + b] = 1
    c = {
        "c_centre": per_image(np.eye(C, dtype=f) - f(1 / C)),
        "c_mean": np.repeat(per_image(np.full((C, 1), 1 / C, f)), E, axis=1),
        "c_spread": spread.reshape(P, QUAD, P),
        "c_eps": np.tile(np.array([EPS_CONV, EPS_FFN, EPS_INST], f), (P, 1)),
        "c_ident": np.eye(P, dtype=f),
        "c_wq": per_image(qkv[0].T), "c_wk": per_image(qkv[1].T), "c_wv": wv.reshape(P, 2, IMG * HALVES * D),
        "c_qb": column(qkv_b[0]), "c_kb": column(qkv_b[1]), "c_vb": column(qkv_b[2]),
        "c_wp": per_image(w["conv_proj_w"].T), "c_pb": column(w["conv_proj_b"]),
        "c_nw": column(w["conv_norm_w"]), "c_nb": column(w["conv_norm_b"]),
        "c_masks": masks.reshape(P, IMG + HEADS),
        "c_router": per_image(w["ffn_router_w"]), "c_rb": np.tile(w["ffn_router_b"], P // E).reshape(P, 1),
        "c_rank": np.tile(np.arange(E, 0, -1, dtype=f), (P, 1)),
        "s_gate": gate.reshape(P, 2 * IMG * P),
        "c_we": w["ffn_expert_w"].reshape(2, P, C).transpose(1, 0, 2),
        "c_eb": eb.reshape(P, QUAD, P),
    }
    return {"x": np.asarray(i["x"]), **c}


def kernel(**inputs):
    import numpy as _np
    import concourse.bacc as _bacc
    from concourse import mybir as _mybir
    from concourse.bass_utils import run_bass_kernel_spmd as _run

    nc = _bacc.Bacc("TRN2", target_bir_lowering=False, num_devices=1)
    arrays = {n: _np.ascontiguousarray(a) for n, a in _layout(inputs).items()}
    io = {n: nc.dram_tensor(n if n != "x" else "in_x", a.shape, _mybir.dt.from_np(a.dtype), kind="ExternalInput").ap()
          for n, a in arrays.items()}
    io["out"] = nc.dram_tensor("out_0", (B, C, H, W), _mybir.dt.float32, kind="ExternalOutput").ap()
    metaformer_block(nc, io)
    r = _run(nc, [{(n if n != "x" else "in_x"): a for n, a in arrays.items()}], core_ids=[0])
    return r.results[0]["out_0"]
```

```python
from contextlib import ExitStack

import concourse.bass as bass
from concourse import mybir

B, C, H, W = 8, 32, 64, 64
HEADS, WS, E = 4, 8, 8
D = C // HEADS
TOK = WS * WS
NW = W // WS
P = 128
IMG = P // C
GROUPS = B // IMG
CHUNK = WS * W
BANDS = H // WS
CHUNKS = GROUPS * BANDS
QUAD = 4
QUADS = CHUNKS // QUAD
PAIRS = IMG // 2
HALVES = HEADS // 2
SPLITS = 3
SCALE = float(D) ** -0.5
EPS_CONV, EPS_FFN, EPS_INST = 1e-6, 1e-5, 1e-6
WEIGHTS = (("c_centre", (P,)), ("c_mean", (C,)), ("c_spread", (QUAD, P)), ("c_eps", (3,)),
           ("c_wq", (P,)), ("c_wk", (P,)), ("c_wv", (2, IMG * C // 2)), ("c_qb", (1,)), ("c_kb", (1,)), ("c_vb", (1,)),
           ("c_wp", (P,)), ("c_pb", (1,)), ("c_nw", (1,)), ("c_nb", (1,)), ("c_masks", (IMG + HEADS,)),
           ("c_ident", (P,)), ("c_router", (QUAD, P)), ("c_rb", (1,)), ("c_rank", (E,)),
           ("c_we", (2, C)), ("c_eb", (QUAD, P)))
FAR = -3.0e38

F32 = mybir.dt.float32
BF16 = mybir.dt.bfloat16
ALU = mybir.AluOpType
ACT = mybir.ActivationFunctionType
AX = mybir.AxisListType


def metaformer_block(nc, io):
    x_v = io["x"].rearrange("(g b) c y x -> g (b c) (y x)", b=IMG)
    out_v = io["out"].rearrange("(g b) c (n y) x -> (b c) g n (y x)", b=IMG, y=WS)

    with ExitStack() as ctx:
        def sb(name, shape, dt=F32):
            return ctx.enter_context(nc.sbuf_tensor(name, shape, dt))

        def sem(name):
            return ctx.enter_context(nc.semaphore(name))

        stage = sb("stage", [P, CHUNKS * CHUNK])
        x_win = sb("x_win", [P, CHUNKS * CHUNK])
        act_all = sb("act_all", [P, CHUNKS * CHUNK])
        half = 2 * IMG * CHUNK
        q_img = stage[:, 0:half].rearrange("p (u win b t) -> p u win b t", u=2, win=NW, b=IMG)
        k_head = stage[:, half:2 * half].rearrange("p (u h n) -> p u h n", u=2, h=HEADS)
        x_rep = stage[:, :].rearrange("p (v b j n) -> p v b j n", v=2, b=IMG, j=2)
        t_norm = x_win
        window_work = sb("window_work", [P, 4 * CHUNK])
        shifted = window_work[:, :].rearrange("p (s n) -> p s n", s=4)
        out_sb = sb("out_sb", [P, 2, CHUNK])
        v_cols = sb("v_cols", [P, 2, NW * IMG * HALVES, 2, 2, D])
        v_flat = v_cols[:].rearrange("p u g b n d -> p (u g b n d)")
        squares = sb("squares", [P, QUAD, CHUNK])
        probs = sb("probs", [P, 4, CHUNK])
        scaled = [(shifted if k < IMG else probs)[:, k % IMG, :] for k in range(2 * IMG)]
        std = sb("std", [P, CHUNK])
        rstd = sb("rstd", [P, CHUNK])
        rstd_first = probs[:, :, :].rearrange("p s n -> p (s n)")
        stats = sb("stats", [P, CHUNKS, 6])
        moments = sb("moments", [P, GROUPS, 2])
        inst = sb("inst", [P, 4, GROUPS])
        inst_s = sb("inst_s", [P, CHUNKS])
        inst_t = sb("inst_t", [P, CHUNKS])
        x_cur = sb("x_cur", [P, CHUNK])
        q_sb = sb("q_sb", [P, CHUNK])
        k_sb = sb("k_sb", [P, CHUNK])
        neg_max = sb("neg_max", [P, 4, PAIRS * HEADS])
        gate_f32 = sb("gate_f32", [P, QUADS * CHUNK])
        gate_copy = [q_sb, k_sb]
        o_tok = sb("o_tok", [P, 2, 16, 32])
        o_rden = sb("o_rden", [P, 2, 32])
        o_norm = sb("o_norm", [P, 2, 8, 32])
        o_chan = sb("o_chan", [P, CHUNK])
        gate_parts = sb("gate_parts", [P, SPLITS, CHUNK], BF16)
        gate_rows = sb("gate_rows", [P, QUADS * QUAD * CHUNK], BF16)
        logit, logit_t, g_a, g_b, g_mask1, g_mask2, g_rest, gate_t = (
            v_flat[:, k * CHUNK:(k + 1) * CHUNK] for k in range(8))
        small = sb("small", [P, 9, CHUNK // E])
        weights = sb("weights_sb", [P, io["weights"].shape[1]])
        const, at = {}, 0
        for n, dims in WEIGHTS:
            cols = dims[0] * (dims[1] if len(dims) > 1 else 1)
            const[n] = weights[:, at:at + cols]
            if len(dims) > 1:
                const[n] = const[n].rearrange("p (a n) -> p a n", a=dims[0])
            at += cols
            if n == "c_eps":
                first_cols = at
        gate_in = gate_f32[:, 0:2 * IMG * P]
        gate_sel = sb("gate_sel_sb", [P, 2 * IMG * P], BF16)
        qb_scaled = sb("qb_scaled", [P, 1])
        proj_bias = sb("proj_bias", [P, 1])

        bank = [ctx.enter_context(nc.psum_tensor(f"bank{i}", [P, 512], F32)) for i in range(8)]

        x_loaded = [sem(f"x_loaded{q}") for q in range(QUADS)]
        x_start_loaded = sem("x_start_loaded")
        first_loaded = sem("first_loaded")
        weights_loaded = sem("weights_loaded")
        gate_in_loaded = sem("gate_in_loaded")
        filled = sem("filled")
        x_win_ready = sem("x_win_ready")

        def norm_sems(tag):
            return {n: sem(f"{tag}_{n}") for n in
                    ("centred_ps", "squared", "var_ps", "std_ready", "rstd_ready", "rstd_ps", "normed")}

        ln1, ln2 = norm_sems("ln1"), norm_sems("ln2")
        stats_done = sem("stats_done")
        inst_step = sem("inst_step")
        inst_std = sem("inst_std")
        affine_ready = sem("affine_ready")
        bias_ps = sem("bias_ps")
        biases_ready = sem("biases_ready")
        x_cur_ready = sem("x_cur_ready")
        q_ps = sem("q_ps")
        k_ps = sem("k_ps")
        v_ps = sem("v_ps")
        q_done = sem("q_done")
        k_done = sem("k_done")
        v_done = sem("v_done")
        q_masks = sem("q_masks")
        k_masks = sem("k_masks")
        score_ps = sem("score_ps")
        max_done = sem("max_done")
        shifted_done = sem("shifted_done")
        turned_ps = sem("turned_ps")
        exp_done = sem("exp_done")
        pv_ps = sem("pv_ps")
        o_turned = sem("o_turned")
        o_recip = sem("o_recip")
        o_normed = sem("o_normed")
        o_back = sem("o_back")
        proj_ps = sem("proj_ps")
        x2_done = sem("x2_done")
        logits_ps = sem("logits_ps")
        gate_step = sem("gate_step")
        gate_exp = sem("gate_exp")
        gates_in = [sem(f"gates_in{j}") for j in range(QUAD)]
        x_rep_in = [sem(f"x_rep_in{u}") for u in range(2)]
        x_rep_pool = sem("x_rep_pool")
        gate_ps = sem("gate_ps")
        scaled_done = sem("scaled_done")
        gate_copied = sem("gate_copied")
        pool_scaled = sem("pool_scaled")
        y_step = sem("y_step")
        summed = sem("summed")
        stored = sem("stored")
        out_free = sem("out_free")

        XC, NORMED, X2, SH, EXP, OT, SC, Y, PS, SUM, OUT, ONE = 2, 4, 3, 2, 2, 2, 2, 2, 2, 2, 2, 1
        GATE_OPS = 26
        POOL_IMAGES = 1
        REPEATS = (IMG * IMG * 16, (IMG - POOL_IMAGES) * IMG * 16)
        DVE_UNITS = 2 * IMG - 2
        ACT_STEPS = (0, 21, 22, 24)

        block = ctx.enter_context(nc.Block())

        @block.sync
        def _(sp):
            per = BANDS // QUAD
            start = 2 * CHUNK
            sp.dma_start(stage[:, 0:start], x_v[0, :, 0:start]).then_inc(x_start_loaded, 16)
            for q in range(QUADS):
                skip = start if q == 0 else 0
                sp.dma_start(stage[:, q * QUAD * CHUNK + skip:(q + 1) * QUAD * CHUNK],
                             x_v[q // per, :, (q % per) * QUAD * CHUNK + skip:(q % per + 1) * QUAD * CHUNK]
                             ).then_inc(x_loaded[q], 16)

            def move_gates(ats):
                for j, at in enumerate(ats):
                    for s in range(SPLITS):
                        sp.dma_start(gate_rows[32 * s:32 * s + 32, bass.ds(at, CHUNK)],
                                     gate_parts[32 * j:32 * j + 32, s, :]).then_inc(gates_in[j], 16)

            def repeat_tokens(at, pair):
                for b in range(IMG if pair == 0 else IMG - POOL_IMAGES):
                    for e in range(IMG):
                        sp.dma_start(x_rep[32 * e:32 * e + 32, pair, b, :, :].rearrange("p j n -> p (j n)"),
                                     t_norm[32 * b:32 * b + 32, bass.ds(at, 2 * CHUNK)]).then_inc(x_rep_in[pair], 16)

            first = [j * CHUNK for j in range(QUAD)]
            sp.wait_ge(ln2["normed"], QUAD + NORMED)
            repeat_tokens(first[0], 0)
            repeat_tokens(first[2], 1)
            sp.wait_ge(filled, 4)
            sp.wait_ge(gate_step, GATE_OPS + ONE)
            move_gates(first)
            with sp.Fori(0, QUADS - 1) as q:
                used0, used1 = sp.snap(q * (2 * QUAD) + (4 + Y)), sp.snap(q * (2 * QUAD) + (8 + Y))
                split = sp.snap(q * GATE_OPS + (2 * GATE_OPS + ONE))
                ats = [sp.snap(q * (QUAD * CHUNK) + (QUAD + j) * CHUNK) for j in range(QUAD)]
                sp.wait_ge(y_step, used0)
                repeat_tokens(ats[0], 0)
                sp.wait_ge(gate_step, split)
                move_gates(ats)
                sp.wait_ge(y_step, used1)
                repeat_tokens(ats[2], 1)

        @block.gpsimd
        def _(pool):
            pool.sem_inc(out_free, OUT)
            pool.sem_inc(pool_scaled, PS)
            pool.memset(v_flat, 0.0).then_inc(filled, 1)
            pool.wait_ge(filled, 1)
            for b in range(2):
                pool.memset(v_cols[b * 64:b * 64 + 64, :, :, b, 1, :].rearrange("p u g d -> p (u g) d"),
                            1.0).then_inc(filled, 1)
                pool.wait_ge(filled, 2 + b)
            pool.wait_ge(x_start_loaded, 16)
            for q in range(QUADS):
                pool.wait_ge(x_loaded[q], 16)
                with pool.Fori(q * QUAD, (q + 1) * QUAD) as c:
                    pool.tensor_copy(
                        x_win[:, bass.ds(c * CHUNK, CHUNK)].rearrange("p (win y x) -> p win y x", win=NW, y=WS),
                        stage[:, bass.ds(c * CHUNK, CHUNK)].rearrange("p (y win x) -> p win y x", win=NW, y=WS),
                    ).then_inc(x_win_ready, 1)
            pool.memset(gate_rows[:, :], 0.0).then_inc(filled, 1)

            def scale(quad, j, i):
                c = quad * QUAD + j
                if j % 2 == 0 and i == 0:
                    pool.wait_ge(x_rep_in[j // 2], quad * REPEATS[j // 2] + REPEATS[j // 2])
                pool.wait_ge(gate_copied, c * 2 + (i + 1))
                pool.wait_ge(y_step, c * 2 + (i + 1))
                pool.tensor_tensor(scaled[i * IMG], x_rep[:, j // 2, 0, j % 2, :], gate_copy[i][:, :],
                                   ALU.mult).then_inc(pool_scaled, 1)

            def store(quad, half, j):
                c = quad * (2 * QUAD) + (half * QUAD + j)
                pool.wait_ge(summed, c + (1 + SUM))
                pool.dma_start(out_v[:, bass.ds(quad, 1), half * QUAD + j, :].rearrange("p a n -> p (a n)"),
                               out_sb[:, j % 2, :]).then_inc(stored, 16)

            def left(quad, half, j):
                pool.wait_ge(stored, quad * (2 * QUAD * 16) + (half * QUAD + j + 1) * 16)
                pool.sem_inc(out_free, 1)

            def repeat_tokens(quad, b):
                at = (quad * QUAD + 2) * CHUNK
                pool.wait_ge(y_step, quad * (2 * QUAD) + Y)
                for e in range(IMG):
                    pool.dma_start(x_rep[32 * e:32 * e + 32, 1, b, :, :].rearrange("p j n -> p (j n)"),
                                   t_norm[32 * b:32 * b + 32, bass.ds(at, 2 * CHUNK)]).then_inc(x_rep_pool, 16)

            with pool.Fori(0, QUADS // 2) as i:
                for u in range(2):
                    for j in range(QUAD):
                        scale(i * 2 + u, j, 0)
                        if j >= 1:
                            store(i, u, j - 1)
                        scale(i * 2 + u, j, 1)
                        if j >= 1:
                            left(i, u, j - 1)
                        if j == 0 and u == 1:
                            left(i, 0, QUAD - 1)
                        if j < POOL_IMAGES:
                            repeat_tokens(i * 2 + u, IMG - 1 - j)
                    store(i, u, QUAD - 1)
                left(i, 1, QUAD - 1)

        def cols(half):
            return slice(0, CHUNK) if half is None else slice(half * CHUNK // 2, (half + 1) * CHUNK // 2)

        def centre(pe, sems, quad, j, source, half=None):
            c = quad * QUAD + j
            if half != 1:
                pe.wait_ge(sems["squared"], c + 1)
            one = nc.tensor.matmul(bank[j % 2][:, cols(half)], const["c_centre"][:, :], source(c, half),
                                   start=True, stop=True)
            if half != 0:
                one.then_inc(sems["centred_ps"], 1)

        def variances(pe, sems, quad, at=2):
            pe.wait_ge(sems["std_ready"], quad + ONE)
            pe.wait_ge(sems["squared"], quad * QUAD + (QUAD + XC))
            for j in range(QUAD):
                last = nc.tensor.matmul(bank[at][32 * j:32 * j + 32, :], const["c_mean"][:, :], squares[:, j, :],
                                        start=True, stop=True)
            last.then_inc(sems["var_ps"], 1)

        def spread(pe, sems, quad, j, banks, half=None, rhs=None):
            c = quad * QUAD + j
            if j == 0:
                pe.wait_ge(sems["rstd_ready"], quad + (1 + ONE))
            if half != 1:
                pe.wait_ge(sems["normed"], c + (1 + NORMED - len(banks)))
            one = nc.tensor.matmul(bank[banks[j % len(banks)]][:, cols(half)], const["c_spread"][:, j, :],
                                   rstd[:, cols(half)] if rhs is None else rhs, start=True, stop=True)
            if half != 0:
                one.then_inc(sems["rstd_ps"], 1)

        def square(act, sems, quad, j, target):
            c = quad * QUAD + j
            act.wait_ge(sems["centred_ps"], c + 1)
            nc.scalar.activation(target[:, bass.ds(c * CHUNK, CHUNK)], bank[j % 2][:, :], ACT.Copy)
            if j == 0:
                act.wait_ge(sems["var_ps"], quad + ONE)
            nc.scalar.activation(squares[:, j, :], bank[j % 2][:, :], ACT.Square).then_inc(sems["squared"], 1)

        def deviations(act, sems, quad, eps, at=2):
            act.wait_ge(sems["var_ps"], quad + (1 + ONE))
            act.wait_ge(sems["rstd_ready"], quad + ONE)
            nc.scalar.activation(std[:, :], bank[at][:, :], ACT.Sqrt, bias=eps).then_inc(sems["std_ready"], 1)

        def reciprocals(dve, sems, quad):
            dve.wait_ge(sems["std_ready"], quad + (1 + ONE))
            dve.wait_ge(sems["rstd_ps"], quad * QUAD + ONE)
            nc.vector.reciprocal(rstd[:, :], std[:, :]).then_inc(sems["rstd_ready"], 1)

        def normalise(dve, sems, quad, j, target, banks):
            c = quad * QUAD + j
            at = bass.ds(c * CHUNK, CHUNK)
            dve.wait_ge(sems["rstd_ps"], c + (1 + ONE))
            nc.vector.tensor_tensor(target[:, at], target[:, at], bank[banks[j % len(banks)]][:, :],
                                    ALU.mult).then_inc(sems["normed"], 1)

        LN1_BANKS, LN2_BANKS, LN2_FIRST = (3, 4, 5, 6), (3, 0, 1), (1, 3)

        def gate_bank(k, deep):
            return bank[(4, 5, 0, 1)[k % 4] if deep else 4 + k % 2][:, :]

        @block.tensor
        def _(pe):
            for s, k in ((proj_ps, ONE), (ln1["var_ps"], ONE), (ln2["var_ps"], ONE),
                         (ln1["rstd_ps"], ONE), (ln2["rstd_ps"], ONE)):
                pe.sem_inc(s, k)
            pe.sem_inc(y_step, Y)

            def natural(c, half):
                return stage[:, bass.ds(c * CHUNK, CHUNK)].rearrange("p (y win x) -> p win y x", win=NW, y=WS)

            def spread_first(quad, j):
                spread(pe, ln1, quad, j, LN1_BANKS, rhs=rstd_first[:, bass.ds(quad * CHUNK, CHUNK)])

            pe.wait_ge(first_loaded, 16)
            for q in range(2):
                for j in range(QUAD):
                    if q == 0 and j == 0:
                        pe.wait_ge(x_start_loaded, 16)
                    if j == (2 if q == 0 else 0):
                        pe.wait_ge(x_loaded[q], 16)
                    centre(pe, ln1, q, j, natural)
                variances(pe, ln1, q)
            for q in range(2, QUADS):
                pe.wait_ge(x_loaded[q], 16)
            with pe.Fori(0, QUADS - 2) as q:
                for j in range(QUAD):
                    spread_first(q, j)
                    centre(pe, ln1, q + 2, j, natural)
                variances(pe, ln1, q + 2)
            pe.wait_ge(weights_loaded, 16)
            nc.tensor.matmul(bank[7][:, 0:1], const["c_wp"][:, :], const["c_vb"][:, :],
                             start=True, stop=True).then_inc(bias_ps, 1)

            def queries(m):
                pe.wait_ge(x_cur_ready, m + 1)
                pe.wait_ge(x2_done, m + 1)
                nc.tensor.matmul(bank[0][:, :], const["c_wq"][:, :], x_cur[:, :],
                                 start=True, stop=True).then_inc(q_ps, 1)

            def keys(m):
                pe.wait_ge(q_done, m + 1)
                nc.tensor.matmul(bank[0][:, :], const["c_wk"][:, :], x_cur[:, :],
                                 start=True, stop=True).then_inc(k_ps, 1)

            def values(m, first=False):
                if not first:
                    pe.wait_ge(v_done, m * 2)
                for w in range(NW):
                    for hl in range(2):
                        last = nc.tensor.matmul(bank[1][64 * hl:64 * hl + 64, w * 64:w * 64 + 64],
                                                x_cur[:, w * TOK:w * TOK + TOK], const["c_wv"][:, hl, :],
                                                start=True, stop=True)
                last.then_inc(v_ps, 1)

            def score(m, u, w):
                if w == 0:
                    pe.wait_ge(q_masks, m + 1)
                    pe.wait_ge(k_masks, m + 1)
                pe.wait_ge(shifted_done, m * NW + (w + 1))
                for p in range(PAIRS):
                    last = nc.tensor.matmul(bank[2 + w % 2][:, p * 256:p * 256 + 256],
                                            q_img[:, u, w, 2 * p:2 * p + 2, :].rearrange("p b t -> p (b t)"),
                                            k_head[:, u, :, w * TOK:w * TOK + TOK], start=True, stop=True)
                last.then_inc(score_ps, 1)

            def turn(n, w):
                pe.wait_ge(shifted_done, n * NW + (w + 1 + SH))
                pe.wait_ge(exp_done, n * NW + (w + 1))
                for k in range(PAIRS * HALVES):
                    last = nc.tensor.transpose(bank[4 + w % 2][:, k * P:k * P + P],
                                               shifted[:, w % 4, k * P:k * P + P], const["c_ident"][:, :])
                last.then_inc(turned_ps, 1)

            def weigh(n, u, w):
                if w == 0:
                    pe.wait_ge(v_done, n * 2 + 2)
                if w % 4 == 0:
                    pe.wait_ge(o_turned, n * 2 + (w // 4 + 1))
                pe.wait_ge(exp_done, n * NW + (w + 1 + EXP))
                for b in range(IMG):
                    for hh in range(HALVES):
                        at, k = hh * 256 + (w % 4) * TOK, (b // 2) * HALVES + hh
                        last = nc.tensor.matmul(
                            bank[6 + w // 4][32 * b:32 * b + 32, at:at + TOK],
                            v_cols[:, u, (w * IMG + b) * HALVES + hh, :, :, :].rearrange("p b n d -> p (b n d)"),
                            probs[:, w % 4, k * P + (b % 2) * TOK:k * P + (b % 2) * TOK + TOK],
                            start=True, stop=True)
                last.then_inc(pv_ps, 1)

            def project(n, k_waits, at=0):
                pe.wait_ge(o_back, n * 2 + 2)
                pe.wait_ge(k_done, k_waits)
                nc.tensor.matmul(bank[at][:, :], const["c_wp"][:, :], o_chan[:, :],
                                 start=True, stop=True).then_inc(proj_ps, 1)

            def tokens(c, half):
                at = cols(half)
                return act_all[:, bass.ds(c * CHUNK + at.start, at.stop - at.start)]

            def chunk(m, u, first=False, final=False):
                for w in range(NW):
                    score(m, u, w)
                    if not final:
                        if w == 1:
                            queries(m + 1)
                        if w == 2:
                            keys(m + 1)
                    if w >= 2:
                        turn(m, w - 2)
                    elif not first:
                        turn(m - 1, w - 2 + NW)
                    if w >= 3:
                        weigh(m, u, w - 3)
                    elif not first:
                        weigh(m - 1, 1 - u, w - 3 + NW)
                    if w == 4 and not final:
                        values(m + 1)
                    if final and w == 1:
                        pe.wait_ge(x2_done, CHUNKS - 2 + X2)
                        pe.wait_ge(v_done, CHUNKS * 2)
                    if final and w in (1, 2):
                        centre(pe, ln2, 0, 2 * w - 2, tokens)
                        centre(pe, ln2, 0, 2 * w - 1, tokens)
                    if final and w == 3:
                        variances(pe, ln2, 0, at=1)
                    if final and w == 7:
                        spread(pe, ln2, 0, 0, LN2_FIRST)
                    if w == 6 and not first:
                        project(m - 1, CHUNKS if final else m + 2)

            for j in range(QUAD):
                spread_first(QUADS - 2, j)
            queries(0)
            keys(0)
            values(0, first=True)
            for j in range(QUAD):
                spread_first(QUADS - 1, j)
            pe.wait_ge(biases_ready, 1)
            chunk(0, 0, first=True)
            with pe.Fori(0, CHUNKS // 2 - 1) as i:
                chunk(i * 2 + 1, 1)
                chunk(i * 2 + 2, 0)
            chunk(CHUNKS - 1, 1, final=True)
            turn(CHUNKS - 1, NW - 2)
            weigh(CHUNKS - 1, 1, NW - 3)
            turn(CHUNKS - 1, NW - 1)
            weigh(CHUNKS - 1, 1, NW - 2)
            for j in (1, 2):
                spread(pe, ln2, 0, j, LN2_FIRST)
            weigh(CHUNKS - 1, 1, NW - 1)
            spread(pe, ln2, 0, 3, LN2_FIRST)

            def router(quad, j, half=None):
                pe.wait_ge(ln2["normed"], quad * QUAD + (j + 1 + NORMED))
                if j == 0 and half != 1:
                    pe.wait_ge(ln2["std_ready"], quad + (1 + ONE))
                at = cols(half)
                one = nc.tensor.matmul(bank[2][:, at], const["c_router"][:, j, :],
                                       t_norm[:, bass.ds((quad * QUAD + j) * CHUNK + at.start, at.stop - at.start)],
                                       start=(j == 0), stop=(j == QUAD - 1), skip_group_check=True)
                if j == QUAD - 1 and half != 0:
                    one.then_inc(logits_ps, 1)

            def spread_gates(quad, j, k, deep, enter):
                c = quad * QUAD + j
                at = c * CHUNK
                if deep and not (enter and k < 2):
                    if k % IMG == 0:
                        pe.wait_ge(gate_copied, c * 2 + k // IMG)
                    else:
                        pe.wait_ge(scaled_done, c * DVE_UNITS + {1: 0, 2: 1, 3: 2, 5: 3, 6: 4, 7: 5}[k])
                elif k in (2, 6):
                    pe.wait_ge(gate_copied, c * 2 + (k // IMG + 1))
                else:
                    pe.wait_ge(scaled_done, c * DVE_UNITS + {0: 1, 1: 2, 3: 3, 4: 4, 5: 5, 7: 6}[k])
                nc.tensor.matmul(gate_bank(k, deep), gate_sel[:, k * P:(k + 1) * P], gate_rows[:, bass.ds(at, CHUNK)],
                                 start=True, stop=True).then_inc(gate_ps, 1)

            def experts(quad, j, eh):
                pe.wait_ge(scaled_done, (quad * QUAD + j) * DVE_UNITS + (DVE_UNITS // 2 * (eh + 1) + SC))
                pe.wait_ge(pool_scaled, (quad * QUAD + j) * 2 + (eh + 1 + PS))
                for b in range(IMG):
                    last = nc.tensor.matmul(bank[6 + j % 2][32 * b:32 * b + 32, :], const["c_we"][:, eh, :],
                                            scaled[eh * IMG + b], start=False, stop=(eh == 1),
                                            skip_group_check=True)
                last.then_inc(y_step, 1)

            def bias(quad, j):
                pe.wait_ge(summed, quad * QUAD + (j + 1))
                nc.tensor.matmul(bank[6 + j % 2][:, :], const["c_eb"][:, j, :],
                                 gate_f32[:, bass.ds(quad * CHUNK, CHUNK)],
                                 start=True, stop=False, skip_group_check=True)

            def next_norm(quad, at):
                if at < 2 * QUAD:
                    centre(pe, ln2, quad, at // 2, tokens, half=at % 2)
                if at == 8:
                    pe.wait_ge(gate_step, (quad - 1) * GATE_OPS + (1 + ONE))
                    variances(pe, ln2, quad)
                if 0 <= at - 11 < 2 * QUAD:
                    spread(pe, ln2, quad, (at - 11) // 2, LN2_BANKS, half=(at - 11) % 2)
                if 0 <= at - 20 < 2 * QUAD:
                    router(quad, (at - 20) % QUAD, half=(at - 20) // QUAD)

            def mixture(quad, norm_next=False, enter=False):
                late = 0 if norm_next else 1
                for j in range(QUAD):
                    pe.wait_ge(gates_in[j], quad * (SPLITS * 16) + SPLITS * 16)
                    for k in range(2 * IMG):
                        spread_gates(quad, j, k, not norm_next, enter and j == 0)
                        if k == 1 + late and j >= 1:
                            experts(quad, j - 1, 1)
                        if k == 3:
                            bias(quad, j)
                        if k == 5 + late:
                            experts(quad, j, 0)
                        if norm_next:
                            next_norm(quad + 2, j * 2 * IMG + k)
                experts(quad, QUAD - 1, 1)

            for j in range(QUAD):
                router(0, j)
            project(CHUNKS - 1, CHUNKS, at=5)
            pe.wait_ge(x2_done, CHUNKS - 1 + X2)
            for j in range(QUAD):
                centre(pe, ln2, 1, j, tokens)
            pe.wait_ge(gate_step, 1 + ONE)
            variances(pe, ln2, 1)
            for j in range(QUAD):
                spread(pe, ln2, 1, j, LN2_BANKS)
            for j in range(QUAD):
                router(1, j)
            pe.wait_ge(x2_done, CHUNKS + X2)
            with pe.Fori(0, QUADS - 2) as q:
                mixture(q, norm_next=True)
            mixture(QUADS - 2, enter=True)
            mixture(QUADS - 1)

        @block.scalar
        def _(act):
            for sems in (ln1, ln2):
                act.sem_inc(sems["squared"], XC)
                act.sem_inc(sems["std_ready"], ONE)
            act.sem_inc(exp_done, EXP)
            act.dma_start(weights[:, 0:first_cols], io["weights"][:, 0:first_cols]).then_inc(first_loaded, 16)
            act.dma_start(weights[:, first_cols:], io["weights"][:, first_cols:]).then_inc(weights_loaded, 16)
            act.dma_start(gate_in, io["gate_sel"]).then_inc(gate_in_loaded, 16)
            act.wait_ge(first_loaded, 16)

            nc.scalar.activation(std[:, 0:3], const["c_eps"][:, :], ACT.Sqrt)

            def first_norm(quad):
                for j in range(QUAD):
                    square(act, ln1, quad, j, act_all)
                deviations(act, ln1, quad, const["c_eps"][:, 0:1])

            first_norm(0)
            first_norm(1)
            with act.Fori(0, QUADS - 2) as q:
                first_norm(q + 2)

            def instance_deviation(g):
                act.wait_ge(inst_step, g * 4 + 1)
                nc.scalar.activation(inst[:, 0, g:g + 1], moments[:, g, 1:2], ACT.Sqrt, bias=const["c_eps"][:, 2:3]
                                     ).then_inc(inst_std, 1)

            def current(m):
                nc.scalar.activation(x_cur[:, :], act_all[:, bass.ds(m * CHUNK, CHUNK)], ACT.Identity,
                                     bias=inst_t[:, bass.ds(m, 1)], scale=inst_s[:, bass.ds(m, 1)]
                                     ).then_inc(x_cur_ready, 1)

            def copy_queries(m):
                act.wait_ge(q_ps, m + 1)
                act.wait_ge(q_masks, m)
                nc.scalar.activation(q_sb[:, :], bank[0][:, :], ACT.Identity, bias=qb_scaled[:, 0:1],
                                     scale=SCALE).then_inc(q_done, 1)

            def copy_keys(m):
                act.wait_ge(k_ps, m + 1)
                act.wait_ge(k_masks, m)
                nc.scalar.activation(k_sb[:, :], bank[0][:, :], ACT.Identity,
                                     bias=const["c_kb"][:, 0:1]).then_inc(k_done, 1)

            def mask_queries(m, u, b):
                if b == 0:
                    act.wait_ge(q_done, m + 1)
                one = nc.scalar.activation(q_img[:, u, :, b, :], q_sb[:, :].rearrange("p (win t) -> p win t", win=NW),
                                           ACT.Copy, scale=const["c_masks"][:, b:b + 1])
                if b == IMG - 1:
                    one.then_inc(q_masks, 1)

            def mask_keys(m, u, h):
                if h == 0:
                    act.wait_ge(k_done, m + 1)
                one = nc.scalar.activation(k_head[:, u, h, :], k_sb[:, :], ACT.Copy,
                                           scale=const["c_masks"][:, IMG + h:IMG + h + 1])
                if h == HEADS - 1:
                    one.then_inc(k_masks, 1)

            def copy_values(m, u):
                act.wait_ge(v_ps, m + 1)
                for hl in range(2):
                    nc.scalar.activation(v_cols[64 * hl:64 * hl + 64, u, :, hl, 0, :],
                                         bank[1][64 * hl:64 * hl + 64, :].rearrange("p (g d) -> p g d", d=D),
                                         ACT.Copy).then_inc(v_done, 1)

            def exps(n, w):
                act.wait_ge(turned_ps, n * NW + (w + 1))
                nc.scalar.activation(probs[:, w % 4, :], bank[4 + w % 2][:, :], ACT.Exp).then_inc(exp_done, 1)

            def chunk(m, u, first=False, final=False):
                for w in range(NW):
                    if w == 0 and not final:
                        current(m + 1)
                    if w >= 2:
                        exps(m, w - 2)
                    elif not first:
                        exps(m - 1, w - 2 + NW)
                    if not final:
                        if w == 1:
                            copy_queries(m + 1)
                        if w == 2:
                            copy_keys(m + 1)
                        for k in range(2):
                            if w in (3, 4):
                                mask_queries(m + 1, 1 - u, 2 * (w - 3) + k)
                            if w in (5, 6):
                                mask_keys(m + 1, 1 - u, 2 * (w - 5) + k)
                        if w == 7:
                            copy_values(m + 1, 1 - u)
                    if final and w in (1, 2):
                        square(act, ln2, 0, 2 * w - 2, t_norm)
                        square(act, ln2, 0, 2 * w - 1, t_norm)
                    if final and w == 4:
                        deviations(act, ln2, 0, const["c_eps"][:, 1:2], at=1)

            instance_deviation(0)
            act.wait_ge(affine_ready, 1)
            current(0)
            copy_queries(0)
            act.wait_ge(x_win_ready, CHUNKS)
            for b in range(IMG):
                mask_queries(0, 0, b)
            copy_keys(0)
            for h in range(HEADS):
                mask_keys(0, 0, h)
            act.wait_ge(filled, 3)
            copy_values(0, 0)
            instance_deviation(1)
            chunk(0, 0, first=True)
            with act.Fori(0, CHUNKS // 2 - 1) as i:
                chunk(i * 2 + 1, 1)
                chunk(i * 2 + 2, 0)
            chunk(CHUNKS - 1, 1, final=True)
            exps(CHUNKS - 1, NW - 2)
            exps(CHUNKS - 1, NW - 1)

            def layer_norm(quad):
                for j in range(QUAD):
                    square(act, ln2, quad, j, t_norm)
                deviations(act, ln2, quad, const["c_eps"][:, 1:2])

            def gate_exps(quad):
                act.wait_ge(gate_step, quad * GATE_OPS + (10 + ONE))
                nc.scalar.activation(small[:, 5, :], small[:, 4, :], ACT.Exp).then_inc(gate_exp, 1)

            def gate_logits(quad):
                act.wait_ge(logits_ps, quad + 1)
                nc.scalar.activation(logit, bank[2][:, :], ACT.Identity, bias=const["c_rb"][:, 0:1]
                                     ).then_inc(gate_step, 1)

            def gate_copies(quad, step, first=False):
                if step != 22:
                    act.wait_ge(gate_step, quad * GATE_OPS + (step + ONE))
                if step == 22 and not first:
                    for j in range(QUAD):
                        act.wait_ge(gates_in[j], quad * (SPLITS * 16))
                if step == 21:
                    one = nc.scalar.activation(gate_f32[:, bass.ds(quad * CHUNK, CHUNK)], g_rest, ACT.Copy)
                if step == 22:
                    one = nc.scalar.activation(gate_parts[:, 0, :], g_rest, ACT.Copy)
                if step == 24:
                    one = nc.scalar.activation(gate_parts[:, 1, :], g_a, ACT.Copy)
                one.then_inc(gate_step, 1)

            def copy_gates(quad, j, i):
                c = quad * QUAD + j
                act.wait_ge(gate_ps, c * 8 + (i * IMG + 1))
                act.wait_ge(pool_scaled, c * 2 + (i + 1))
                nc.scalar.activation(gate_copy[i][:, :], bank[4][:, :], ACT.Copy).then_inc(gate_copied, 1)

            def mixture(quad, gate_next=False, norm_next=False):
                if gate_next:
                    gate_logits(quad + 1)
                for j in range(QUAD):
                    for i in range(2):
                        copy_gates(quad, j, i)
                        if norm_next and j == 0:
                            square(act, ln2, quad + 2, 2 * i, t_norm)
                            square(act, ln2, quad + 2, 2 * i + 1, t_norm)
                        if norm_next and (j, i) == (1, 0):
                            deviations(act, ln2, quad + 2, const["c_eps"][:, 1:2])
                        if gate_next and (j, i) == (1, 0):
                            gate_exps(quad + 1)
                        if gate_next and (j, i) == (2, 1):
                            for step in (21, 22, 24):
                                gate_copies(quad + 1, step)

            gate_logits(0)
            layer_norm(1)
            gate_exps(0)
            for step in (21, 22, 24):
                gate_copies(0, step, first=True)
            with act.Fori(0, QUADS - 2) as q:
                mixture(q, gate_next=True, norm_next=True)
            mixture(QUADS - 2, gate_next=True)
            mixture(QUADS - 1)

        @block.vector
        def _(dve):
            for s, k in ((ln1["normed"], NORMED), (ln2["normed"], NORMED), (x2_done, X2), (o_turned, OT),
                         (shifted_done, SH), (scaled_done, SC), (summed, SUM), (gate_step, ONE),
                         (ln1["rstd_ready"], ONE), (ln2["rstd_ready"], ONE)):
                dve.sem_inc(s, k)
            def statistics(c):
                dve.wait_ge(ln1["normed"], c + (1 + NORMED))
                nc.vector.bn_stats(stats[:, bass.ds(c, 1), :].rearrange("p a s -> p (a s)"),
                                   act_all[:, bass.ds(c * CHUNK, CHUNK)]).then_inc(stats_done, 1)

            def instance_moments(g):
                dve.wait_ge(stats_done, (g + 1) * BANDS)
                nc.vector.bn_aggr(moments[:, g, :], stats[:, g * BANDS:(g + 1) * BANDS, :]
                                  .rearrange("p n s -> p (n s)")).then_inc(inst_step, 1)

            def instance_affine(g):
                dve.wait_ge(inst_std, g + 1)
                nc.vector.reciprocal(inst[:, 1, g:g + 1], inst[:, 0, g:g + 1]).then_inc(inst_step, 1)
                dve.wait_ge(inst_step, g * 4 + 2)
                nc.vector.tensor_scalar(inst[:, 2, g:g + 1], inst[:, 1, g:g + 1], const["c_nw"][:, 0:1], None,
                                        ALU.mult).then_inc(inst_step, 1)
                dve.wait_ge(inst_step, g * 4 + 3)
                nc.vector.tensor_tensor(inst[:, 3, g:g + 1], moments[:, g, 0:1], inst[:, 2, g:g + 1],
                                        ALU.mult).then_inc(inst_step, 1)
                dve.wait_ge(inst_step, g * 4 + 4)
                at = slice(g * BANDS, (g + 1) * BANDS)
                nc.vector.tensor_copy(inst_s[:, at], inst[:, 2, g:g + 1].to_broadcast([P, BANDS]))
                nc.vector.tensor_scalar(inst_t[:, at], inst[:, 3, g:g + 1].to_broadcast([P, BANDS]),
                                        -1.0, const["c_nb"][:, 0:1], ALU.mult, ALU.add).then_inc(affine_ready, 1)

            def first_norm(quad):
                for j in range(QUAD):
                    normalise(dve, ln1, quad, j, act_all, LN1_BANKS)

            def reciprocals_first(quad):
                dve.wait_ge(ln1["std_ready"], quad + (1 + ONE))
                nc.vector.reciprocal(rstd_first[:, bass.ds(quad * CHUNK, CHUNK)], std[:, :]
                                     ).then_inc(ln1["rstd_ready"], 1)

            reciprocals_first(0)
            with dve.Fori(0, QUADS - 2) as q:
                reciprocals_first(q + 1)
                first_norm(q)
                for j in range(QUAD):
                    statistics(q * QUAD + j)
            dve.wait_ge(weights_loaded, 16)
            nc.vector.tensor_scalar(qb_scaled[:, :], const["c_qb"][:, :], SCALE, None, ALU.mult)
            instance_moments(0)
            reciprocals_first(QUADS - 1)
            instance_affine(0)
            first_norm(QUADS - 2)
            for j in range(QUAD):
                statistics((QUADS - 2) * QUAD + j)
            for j in range(QUAD):
                normalise(dve, ln1, QUADS - 1, j, act_all, LN1_BANKS)
                if j >= 1:
                    statistics((QUADS - 1) * QUAD + j - 1)
            dve.wait_ge(bias_ps, 1)
            nc.vector.tensor_tensor(proj_bias[:, :], bank[7][:, 0:1], const["c_pb"][:, :],
                                    ALU.add).then_inc(biases_ready, 1)
            statistics(CHUNKS - 1)
            instance_moments(1)
            dve.wait_ge(gate_in_loaded, 16)
            nc.vector.tensor_copy(gate_sel[:, :], gate_in)

            def shift(m, w):
                dve.wait_ge(score_ps, m * NW + (w + 1))
                t = bank[2 + w % 2][:, :].rearrange("p (g k) -> p g k", k=TOK)
                nc.vector.tensor_reduce(neg_max[:, w % 4, :], t, AX.X, ALU.max, negate=True).then_inc(max_done, 1)
                dve.wait_ge(max_done, m * NW + (w + 1))
                nc.vector.tensor_tensor(shifted[:, w % 4, :].rearrange("p (g k) -> p g k", k=TOK), t,
                                        neg_max[:, w % 4, :].unsqueeze(2).to_broadcast([P, PAIRS * HEADS, TOK]),
                                        ALU.add).then_inc(shifted_done, 1)

            def divide(n, hf):
                dve.wait_ge(pv_ps, n * NW + (4 * hf + 4))
                t = o_tok[:, hf, :, :]
                nc.vector.transpose(t.rearrange("p g c -> p (g c)"), bank[6 + hf][:, :]).then_inc(o_turned, 1)
                dve.wait_ge(o_turned, n * 2 + (hf + 1 + OT))
                nc.vector.reciprocal(o_rden[:, hf, :], t.rearrange("p g (b n d) -> p (g b) n d", b=2, n=2)[:, :, 1, 0]
                                     ).then_inc(o_recip, 1)
                dve.wait_ge(o_recip, n * 2 + (hf + 1))
                for p in range(PAIRS):
                    last = nc.vector.tensor_tensor(
                        o_norm[:, hf, :, p * 16:p * 16 + 16].rearrange("p g (b d) -> p g b d", b=2),
                        t[:, p * 8:p * 8 + 8, :].rearrange("p g (b n d) -> p g b n d", b=2, n=2)[:, :, :, 0, :],
                        o_rden[:, hf, p * 16:p * 16 + 16].rearrange("p (g b) -> p g b", b=2).unsqueeze(3)
                        .to_broadcast([P, 8, 2, D]), ALU.mult)
                last.then_inc(o_normed, 1)

            def turn_back(n, hf):
                dve.wait_ge(o_normed, n * 2 + (hf + 1))
                dve.wait_ge(proj_ps, n + ONE)
                nc.vector.transpose(o_chan[:, hf * 256:hf * 256 + 256],
                                    o_norm[:, hf, :, :].rearrange("p g c -> p (g c)")).then_inc(o_back, 1)

            def residual(n, bank_at=0):
                dve.wait_ge(proj_ps, n + 1 + ONE)
                at = bass.ds(n * CHUNK, CHUNK)
                nc.vector.scalar_tensor_tensor(out=act_all[:, at], in0=bank[bank_at][:, :], scalar=proj_bias[:, 0:1],
                                               in1=x_win[:, at], op0=ALU.add, op1=ALU.add).then_inc(x2_done, 1)

            def chunk(m, u, first=False, final=False):
                for w in range(NW):
                    shift(m, w)
                    if final and w == 5:
                        reciprocals(dve, ln2, 0)
                    if w == 0 and not first:
                        turn_back(m - 1, 0)
                    if w == 3 and not first:
                        divide(m - 1, 1)
                    if w == 4 and not first:
                        turn_back(m - 1, 1)
                    if first and w == 1:
                        instance_affine(1)
                    if w == NW - 1 and not final:
                        if not first:
                            residual(m - 1)
                        divide(m, 0)

            chunk(0, 0, first=True)
            with dve.Fori(0, CHUNKS // 2 - 1) as i:
                chunk(i * 2 + 1, 1)
                chunk(i * 2 + 2, 0)
            chunk(CHUNKS - 1, 1, final=True)
            for j in range(QUAD):
                normalise(dve, ln2, 0, j, t_norm, LN2_FIRST)
            residual(CHUNKS - 2)
            for hf in range(2):
                divide(CHUNKS - 1, hf)
                turn_back(CHUNKS - 1, hf)

            def wide(k):
                return small[:, k, :].unsqueeze(2).to_broadcast([P, CHUNK // E, E])

            def g(t):
                return t.rearrange("p (g e) -> p g e", e=E)

            v = nc.vector
            rank8 = const["c_rank"][:, :].unsqueeze(1).to_broadcast([P, CHUNK // E, E])
            best, second, best_rank, second_rank, gap, e_gap, total, p_best, p_second = range(9)

            def gates(quad, n):
                dve.wait_ge(gate_step, quad * GATE_OPS + (n + ONE))
                if n == 1:
                    one = v.transpose(logit_t, logit)
                elif n == 2:
                    one = v.tensor_reduce(small[:, best, :], g(logit_t), AX.X, ALU.max)
                elif n == 3:
                    one = v.tensor_tensor(g(g_a), g(logit_t), wide(best), ALU.is_equal)
                elif n == 4:
                    one = v.tensor_tensor(g(g_b), g(g_a), rank8, ALU.mult)
                elif n == 5:
                    one = v.tensor_reduce(small[:, best_rank, :], g(g_b), AX.X, ALU.max)
                elif n == 6:
                    one = v.tensor_tensor(g(g_mask1), g(g_b), wide(best_rank), ALU.is_equal)
                elif n == 7:
                    one = v.scalar_tensor_tensor(out=g_rest, in0=g_mask1, scalar=FAR, in1=logit_t,
                                                 op0=ALU.mult, op1=ALU.add)
                elif n == 8:
                    one = v.tensor_reduce(small[:, second, :], g(g_rest), AX.X, ALU.max)
                elif n == 9:
                    one = v.tensor_tensor(small[:, gap, :], small[:, second, :], small[:, best, :], ALU.subtract)
                elif n == 10:
                    one = v.tensor_tensor(g(g_a), g(g_rest), wide(second), ALU.is_equal)
                elif n == 11:
                    one = v.tensor_tensor(g(g_b), g(g_a), rank8, ALU.mult)
                elif n == 12:
                    one = v.tensor_reduce(small[:, second_rank, :], g(g_b), AX.X, ALU.max)
                elif n == 13:
                    one = v.tensor_tensor(g(g_mask2), g(g_b), wide(second_rank), ALU.is_equal)
                elif n == 14:
                    dve.wait_ge(gate_exp, quad + 1)
                    one = v.tensor_scalar(small[:, total, :], small[:, e_gap, :], 1.0, None, ALU.add)
                elif n == 15:
                    one = v.reciprocal(small[:, p_best, :], small[:, total, :])
                elif n == 16:
                    one = v.tensor_tensor(small[:, p_second, :], small[:, e_gap, :], small[:, p_best, :], ALU.mult)
                elif n == 17:
                    one = v.tensor_tensor(g(g_a), g(g_mask1), wide(p_best), ALU.mult)
                elif n == 18:
                    one = v.tensor_tensor(g(g_b), g(g_mask2), wide(p_second), ALU.mult)
                elif n == 19:
                    one = v.tensor_tensor(gate_t, g_a, g_b, ALU.add)
                elif n == 20:
                    one = v.transpose(g_rest, gate_t)
                elif n == 23:
                    one = v.tensor_tensor(g_a, g_rest, gate_parts[:, 0, :], ALU.subtract)
                elif n == GATE_OPS - 1:
                    one = v.tensor_tensor(gate_parts[:, 2, :], g_a, gate_parts[:, 1, :], ALU.subtract)
                one.then_inc(gate_step, 1)

            def combine(quad, j):
                c = quad * QUAD + j
                dve.wait_ge(y_step, c * 2 + (2 + Y))
                dve.wait_ge(out_free, c + 1)
                nc.vector.tensor_tensor(
                    out_sb[:, j % 2, :].rearrange("p (y win x) -> p win y x", win=NW, y=WS),
                    bank[6 + j % 2][:, :].rearrange("p (win y x) -> p win y x", win=NW, y=WS),
                    act_all[:, bass.ds(c * CHUNK, CHUNK)].rearrange("p (win y x) -> p win y x", win=NW, y=WS),
                    ALU.add).then_inc(summed, 1)

            def mixture(quad, gate_next=False, norm_next=False):
                for j in range(QUAD):
                    c = quad * QUAD + j
                    if j % 2 == 0:
                        dve.wait_ge(x_rep_in[j // 2], quad * REPEATS[j // 2] + REPEATS[j // 2])
                    if j == 2:
                        dve.wait_ge(x_rep_pool, quad * (POOL_IMAGES * IMG * 16) + POOL_IMAGES * IMG * 16)
                    for k in range(2 * IMG):
                        n = j * 2 * IMG + k
                        if k % IMG == 1:
                            dve.wait_ge(y_step, c * 2 + (k // IMG + 1))
                        if k % IMG != 0:
                            dve.wait_ge(gate_ps, c * 8 + (k + 1))
                            nc.vector.tensor_tensor(scaled[k], x_rep[:, j // 2, k % IMG, j % 2, :],
                                                    gate_bank(k, not norm_next), ALU.mult).then_inc(scaled_done, 1)
                        if gate_next and n < GATE_OPS and n not in ACT_STEPS:
                            gates(quad + 1, n)
                        if norm_next and n == 10:
                            reciprocals(dve, ln2, quad + 2)
                        if norm_next and n in (13, 15, 17, 19):
                            normalise(dve, ln2, quad + 2, (n - 13) // 2, t_norm, LN2_BANKS)
                        if k == IMG - 1 and j >= 1:
                            combine(quad, j - 1)
                combine(quad, QUAD - 1)

            for n in range(GATE_OPS):
                if n == 14:
                    residual(CHUNKS - 1, bank_at=5)
                if n == 16:
                    reciprocals(dve, ln2, 1)
                if n not in ACT_STEPS:
                    gates(0, n)
            for j in range(QUAD):
                normalise(dve, ln2, 1, j, t_norm, LN2_BANKS)
            with dve.Fori(0, QUADS - 2) as q:
                mixture(q, gate_next=True, norm_next=True)
            mixture(QUADS - 2, gate_next=True)
            mixture(QUADS - 1)


def _layout(i):
    import numpy as np

    f = np.float32
    eye = np.eye(IMG, dtype=f)
    w = {k[len("L0_"):]: np.asarray(v) for k, v in i.items() if k != "x"}
    qkv = w["conv_qkv_w"].reshape(3, C, C)
    qkv_b = w["conv_qkv_b"].reshape(3, C)

    def per_image(block):
        out = np.zeros((IMG, block.shape[0], IMG, block.shape[1]), f)
        for b in range(IMG):
            out[b, :, b, :] = block
        return out.reshape(IMG * block.shape[0], IMG * block.shape[1])

    def column(v):
        return np.tile(v, IMG).reshape(P, 1)

    wv = np.zeros((IMG, C, 2, IMG, HALVES, D), f)
    for b in range(IMG):
        wv[b, :, :, b] = qkv[2].T.reshape(C, HALVES, 2, D).transpose(0, 2, 1, 3)
    eb = np.zeros((QUAD, IMG, E, QUAD, IMG, C), f)
    for j in range(QUAD):
        for b in range(IMG):
            eb[j, b, :, j, b, :] = w["ffn_expert_b"]
    spread = np.zeros((QUAD, IMG, E, QUAD, IMG, C), f)
    router = np.zeros((IMG, C, QUAD, QUAD, IMG, E), f)
    for b in range(IMG):
        for j in range(QUAD):
            router[b, :, j, j, b, :] = w["ffn_router_w"]
    gate = np.zeros((QUAD, IMG, E, 2, IMG, IMG, C), f)
    for b in range(IMG):
        for j in range(QUAD):
            spread[j, b, 0, j, b, :] = 1
        for e in range(E):
            gate[:SPLITS, b, e, e // 4, b, e % 4, :] = 1
    masks = np.zeros((IMG, HEADS, D, IMG + HEADS), f)
    for b in range(4):
        masks[b, :, :, b] = 1
        masks[:, b, :, IMG + b] = 1
    c = {
        "c_centre": per_image(np.eye(C, dtype=f) - f(1 / C)),
        "c_mean": np.repeat(per_image(np.full((C, 1), 1 / C, f)), E, axis=1),
        "c_spread": spread.reshape(P, QUAD, P),
        "c_eps": np.tile(np.array([EPS_CONV, EPS_FFN, EPS_INST], f), (P, 1)),
        "c_ident": np.eye(P, dtype=f),
        "c_wq": per_image(qkv[0].T), "c_wk": per_image(qkv[1].T), "c_wv": wv.reshape(P, 2, IMG * HALVES * D),
        "c_qb": column(qkv_b[0]), "c_kb": column(qkv_b[1]), "c_vb": column(qkv_b[2]),
        "c_wp": per_image(w["conv_proj_w"].T), "c_pb": column(w["conv_proj_b"]),
        "c_nw": column(w["conv_norm_w"]), "c_nb": column(w["conv_norm_b"]),
        "c_masks": masks.reshape(P, IMG + HEADS),
        "c_router": router.reshape(P, QUAD, P), "c_rb": np.tile(w["ffn_router_b"], P // E).reshape(P, 1),
        "c_rank": np.tile(np.arange(E, 0, -1, dtype=f), (P, 1)),
        "c_we": w["ffn_expert_w"].reshape(2, P, C).transpose(1, 0, 2),
        "c_eb": eb.reshape(P, QUAD, P),
    }
    return {"x": np.asarray(i["x"]), "gate_sel": gate.reshape(P, 2 * IMG * P),
            "weights": np.concatenate([c[n].reshape(P, -1) for n, _ in WEIGHTS], axis=1)}


def kernel(**inputs):
    import numpy as _np
    import concourse.bacc as _bacc
    from concourse import mybir as _mybir
    from concourse.bass_utils import run_bass_kernel_spmd as _run

    nc = _bacc.Bacc("TRN2", target_bir_lowering=False, num_devices=1)
    arrays = {n: _np.ascontiguousarray(a) for n, a in _layout(inputs).items()}
    io = {n: nc.dram_tensor(n if n != "x" else "in_x", a.shape, _mybir.dt.from_np(a.dtype), kind="ExternalInput").ap()
          for n, a in arrays.items()}
    io["out"] = nc.dram_tensor("out_0", (B, C, H, W), _mybir.dt.float32, kind="ExternalOutput").ap()
    metaformer_block(nc, io)
    r = _run(nc, [{(n if n != "x" else "in_x"): a for n, a in arrays.items()}], core_ids=[0])
    return r.results[0]["out_0"]
```
